# Optimizing a Trainium2 kernel written in Bass

```python
import numpy as np
import jax
import jax.numpy as jnp

def _softmax(x, axis=-1):
    return jax.nn.softmax(x, axis=axis)

def _gelu(x):
    return jax.nn.gelu(x, approximate=True)

def _silu(x):
    return jax.nn.silu(x)

def _sigmoid(x):
    return jax.nn.sigmoid(x)

def _layernorm(x, axis=-1, eps=1e-05):
    m = jnp.mean(x, axis=axis, keepdims=True)
    v = jnp.var(x, axis=axis, keepdims=True)
    return (x - m) / jnp.sqrt(v + eps)

def _scatter_add(tgt, idx, src, axis=0):
    return tgt.at[idx].add(src)

def _segment_sum(src, seg, n):
    return jax.ops.segment_sum(src, seg, n)
kernel_name = 'mk_xattn_ffn_d1_seqx_r8_e8f61f'

def setup_inputs(seed: int=0):
    np.random.seed(seed)
    _w = jnp.asarray

    def _rec_inputs():
        import jax
        import jax.numpy as jnp
        _rk = jax.random.key(seed)
        x = -0.0002928 + 1 * jax.random.normal(jax.random.fold_in(_rk, 1), (4, 512, 128), jnp.float32)
        _lenS = 512 - jax.random.randint(jax.random.fold_in(_rk, 7), (4,), 0, max(1, 512 // 4) + 1, jnp.int32)
        _lenS2 = 154 - jax.random.randint(jax.random.fold_in(_rk, 8), (4,), 0, max(1, 154 // 4) + 1, jnp.int32)
        _ctx_1024P = jax.random.normal(jax.random.fold_in(_rk, 11), (4, 16, 128), jnp.float32)
        _ctx_1024c = jax.random.dirichlet(jax.random.fold_in(_rk, 511), 0.3 * jnp.ones((16,), jnp.float32), (4, 154))
        _ctx_1024t = jnp.einsum('bsk,bkd->bsd', _ctx_1024c, _ctx_1024P)
        _ctx_1024t = _ctx_1024t * jax.lax.rsqrt(jnp.mean(jnp.square(_ctx_1024t)) + 1e-12) * 0.953939
        ctx_1024 = -1.39393e-06 + 0.999914 * (_ctx_1024t + 0.3 * jax.random.normal(jax.random.fold_in(_rk, 611), (4, 154, 128), jnp.float32))
        return (x, ctx_1024)
    x, ctx_1024 = _rec_inputs()

    def _L0_xattn_setup():
        import jax, jax.numpy as jnp
        import numpy as np
        D_MODEL = 128
        N_HEADS = 16
        THRESHOLD = 0.8
        key = jax.random.key(seed)
        ks = jax.random.split(key, 12)
        B, L, D = (2, 256, D_MODEL)
        s = 1.0 / np.sqrt(D)
        return {'q_x': jax.random.normal(ks[0], (B, L, D), jnp.float32), 'k_x': jax.random.normal(ks[1], (B, L, D), jnp.float32), 'v_x': jax.random.normal(ks[2], (B, L, D), jnp.float32), 'energy': jax.random.normal(ks[3], (B, L, D), jnp.float32), 'Wq': jax.random.normal(ks[4], (D, D), jnp.float32) * s, 'bq': jnp.zeros((D,), jnp.float32), 'Wk': jax.random.normal(ks[5], (D, D), jnp.float32) * s, 'bk': jnp.zeros((D,), jnp.float32), 'Wv': jax.random.normal(ks[6], (D, D), jnp.float32) * s, 'bv': jnp.zeros((D,), jnp.float32), 'Wo': jax.random.normal(ks[7], (D, D), jnp.float32) * s, 'bo': jnp.zeros((D,), jnp.float32)}
    _L0_xattn_all = _L0_xattn_setup()
    _L0_xattn_in = {k: v for k, v in _L0_xattn_all.items() if k in ('Wq', 'bq', 'Wk', 'bk', 'Wv', 'bv', 'Wo', 'bo')}
    del _L0_xattn_all

    def _L0_ffn_setup():
        import jax, jax.numpy as jnp
        import numpy as np
        D = 128
        H = 256
        E = 8
        TOP_K = 2
        N_SHARED = 1
        B, S = (2, 128)
        key = jax.random.key(seed)
        ks = jax.random.split(key, 12)
        sc = 0.02
        return {'hidden': jax.random.normal(ks[0], (B, S, D), jnp.float32), 'router_w': jax.random.normal(ks[1], (D, E), jnp.float32) * sc, 'router_b': jnp.zeros((E,), jnp.float32), 'sw1': jax.random.normal(ks[2], (D, H), jnp.float32) * sc, 'sb1': jnp.zeros((H,), jnp.float32), 'sw2': jax.random.normal(ks[3], (H, D), jnp.float32) * sc, 'sb2': jnp.zeros((D,), jnp.float32), 'rw1': jax.random.normal(ks[4], (E, D, H), jnp.float32) * sc, 'rb1': jnp.zeros((E, H), jnp.float32), 'rw2': jax.random.normal(ks[5], (E, H, D), jnp.float32) * sc, 'rb2': jnp.zeros((E, D), jnp.float32)}
    _L0_ffn_all = _L0_ffn_setup()
    _L0_ffn_in = {k: v for k, v in _L0_ffn_all.items() if k in ('router_w', 'router_b', 'sw1', 'sb1', 'sw2', 'sb2', 'rw1', 'rb1', 'rw2', 'rb2')}
    del _L0_ffn_all
    return {'x': x, 'ctx_1024': ctx_1024, 'L0_xattn_Wq': _L0_xattn_in['Wq'], 'L0_xattn_bq': _L0_xattn_in['bq'], 'L0_xattn_Wk': _L0_xattn_in['Wk'], 'L0_xattn_bk': _L0_xattn_in['bk'], 'L0_xattn_Wv': _L0_xattn_in['Wv'], 'L0_xattn_bv': _L0_xattn_in['bv'], 'L0_xattn_Wo': _L0_xattn_in['Wo'], 'L0_xattn_bo': _L0_xattn_in['bo'], 'L0_ffn_router_w': _L0_ffn_in['router_w'], 'L0_ffn_router_b': _L0_ffn_in['router_b'], 'L0_ffn_sw1': _L0_ffn_in['sw1'], 'L0_ffn_sb1': _L0_ffn_in['sb1'], 'L0_ffn_sw2': _L0_ffn_in['sw2'], 'L0_ffn_sb2': _L0_ffn_in['sb2'], 'L0_ffn_rw1': _L0_ffn_in['rw1'], 'L0_ffn_rb1': _L0_ffn_in['rb1'], 'L0_ffn_rw2': _L0_ffn_in['rw2'], 'L0_ffn_rb2': _L0_ffn_in['rb2']}

def reference(x, ctx_1024, L0_xattn_Wq, L0_xattn_bq, L0_xattn_Wk, L0_xattn_bk, L0_xattn_Wv, L0_xattn_bv, L0_xattn_Wo, L0_xattn_bo, L0_ffn_router_w, L0_ffn_router_b, L0_ffn_sw1, L0_ffn_sb1, L0_ffn_sw2, L0_ffn_sb2, L0_ffn_rw1, L0_ffn_rb1, L0_ffn_rw2, L0_ffn_rb2):
    import jax
    import jax.numpy as jnp

    def _L0_xattn_ref(q_x, k_x, v_x, energy, Wq, bq, Wk, bk, Wv, bv, Wo, bo):
        import jax, jax.numpy as jnp
        import numpy as np
        D_MODEL = 128
        N_HEADS = 16
        THRESHOLD = 0.8
        B, L, D = q_x.shape
        H = N_HEADS
        Dh = D // H
        Q = (q_x @ Wq + bq).reshape(B, L, H, Dh).transpose(0, 2, 1, 3)
        K = (k_x @ Wk + bk).reshape(B, -1, H, Dh).transpose(0, 2, 1, 3)
        V = (v_x @ Wv + bv).reshape(B, -1, H, Dh).transpose(0, 2, 1, 3)
        sc = jnp.einsum('bhqd,bhkd->bhqk', Q, K) / jnp.sqrt(jnp.float32(Dh))
        mask = jnp.mean(jnp.abs(energy), axis=-1) > THRESHOLD
        sc = jnp.where(mask[:, None, None, :], sc, -jnp.inf)
        w = jnp.nan_to_num(jax.nn.softmax(sc, axis=-1), nan=0.0)
        o = jnp.einsum('bhqk,bhkd->bhqd', w, V).transpose(0, 2, 1, 3).reshape(B, L, D)
        return o @ Wo + bo

    def _L0_ffn_ref(hidden, router_w, router_b, sw1, sb1, sw2, sb2, rw1, rb1, rw2, rb2):
        import jax, jax.numpy as jnp
        import numpy as np
        D = 128
        H = 256
        E = 8
        TOP_K = 2
        N_SHARED = 1
        B, S = (2, 128)
        b, s, d = hidden.shape
        T = b * s
        flat = hidden.reshape(T, d)
        router_logits = flat @ router_w + router_b
        router_probs = jax.nn.softmax(router_logits, axis=-1)
        topk_probs, topk_idx = jax.lax.top_k(router_probs, TOP_K)
        weights = jnp.zeros_like(router_probs).at[jnp.arange(T)[:, None], topk_idx].add(topk_probs)
        sh = jax.nn.gelu(flat @ sw1 + sb1, approximate=False)
        shared_out = (sh @ sw2 + sb2) / N_SHARED
        h1 = jax.nn.gelu(jnp.einsum('td,edh->teh', flat, rw1) + rb1[None], approximate=False)
        expert_out = jnp.einsum('teh,ehd->ted', h1, rw2) + rb2[None]
        mixed = jnp.einsum('ted,te->td', expert_out, weights)
        return (shared_out + mixed).reshape(b, s, d)
    x = x + _L0_xattn_ref(_layernorm(x, axis=-1), ctx_1024, ctx_1024, ctx_1024, L0_xattn_Wq, L0_xattn_bq, L0_xattn_Wk, L0_xattn_bk, L0_xattn_Wv, L0_xattn_bv, L0_xattn_Wo, L0_xattn_bo)
    x = x + _L0_ffn_ref(_layernorm(x, axis=-1), L0_ffn_router_w, L0_ffn_router_b, L0_ffn_sw1, L0_ffn_sb1, L0_ffn_sw2, L0_ffn_sb2, L0_ffn_rw1, L0_ffn_rb1, L0_ffn_rw2, L0_ffn_rb2)
    return x

_drawn_inputs = setup_inputs


def setup_inputs(seed=0):
    import zlib

    import numpy as np

    out = dict(_drawn_inputs(seed))
    spreads = {'L0_xattn_bq': (0.0, 0.1),
     'L0_xattn_bk': (0.0, 0.8),
     'L0_xattn_bv': (0.0, 0.1),
     'L0_xattn_bo': (0.0, 0.1),
     'L0_ffn_router_b': (0.0, 0.766),
     'L0_ffn_sb1': (0.0, 0.597),
     'L0_ffn_sb2': (0.0, 0.1),
     'L0_ffn_rb1': (0.0, 0.8),
     'L0_ffn_rb2': (0.0, 0.406)}
    factors = {'L0_ffn_router_w': 3.293, 'L0_ffn_rw1': 7.604, 'L0_ffn_rw2': 6.863}
    for name, (base, spread) in spreads.items():
        noise = np.random.default_rng([zlib.crc32(name.encode()), seed]).standard_normal(out[name].shape)
        drawn = base * np.exp(spread * noise) if base else spread * noise
        out[name] = jnp.asarray(drawn.astype(out[name].dtype))
    for name, factor in factors.items():
        out[name] = (out[name] * factor).astype(out[name].dtype)
    return out
```

```python
import concourse.bass as bass
from concourse import mybir
from contextlib import ExitStack


def xattn_moe_kernel(nc: bass.Bass, x, ctx_in, Wq, bq, Wk, bk, Wv, bv, Wo, bo, router_w, router_b,
                     sw1, sb1, sw2, sb2, rw1, rb1, rw2, rb2, out):
    f32 = mybir.dt.float32
    f16 = mybir.dt.float16
    ALU = mybir.AluOpType
    ACT = mybir.ActivationFunctionType
    AX = mybir.AxisListType

    B, L, D = x.shape
    KEYS = ctx_in.shape[1]
    H, DH = 16, 8
    G = 4
    SL = H // G
    R = 32
    MAXROW, MASKROW = 24, 25
    KA = 128
    KR = 32
    KB = KEYS - KA
    KP = KA + KR
    T = L // 128
    NT = B * T
    E = rw1.shape[0]
    NE = E + 1
    C = rw1.shape[2] // 128
    EPS = 1e-5
    BIG = 65504.0
    MAXUNIT = 1024.0
    MAXFLOOR = -6.0e7
    WSCALE = 64.0
    THRESHOLD = 102.4
    SCALE = float(DH) ** -0.5
    PR = 6
    UNITS = SL * (G + 1)

    def attention_of(b):
        for s in range(SL):
            for j in range(G + 1):
                yield ("scores", b, s * (G + 1) + j)
                if j == 2 and s > 0:
                    yield ("normalise", b, s - 1)

    def next_batch(b):
        if b < B:
            yield ("norm1", b, 0)
            for s in range(SL):
                yield ("query", b, s)
            for n in range(T * SL):
                yield ("maxima", b, n)
            yield ("maxrows", b, 0)

    def tail_of(b):
        if b >= 0:
            yield ("normalise", b, SL - 1)
            for name in ("turn_o", "project", "norm2", "turn_f", "route", "turn_w", "bias2"):
                yield (name, b, 0)

    def merged(*streams):
        lots = [list(s) for s in streams]
        keyed = [((i + 0.5) / len(lot), k, step) for k, lot in enumerate(lots) for i, step in enumerate(lot)]
        return [step for _, _, step in sorted(keyed, key=lambda it: it[:2])]

    SCHEDULE = list(next_batch(0))
    for b in range(B):
        SCHEDULE += merged(attention_of(b), next_batch(b + 1), tail_of(b - 1))
        SCHEDULE.append(("last_pv", b, 0)) if b == B - 1 else None
    SCHEDULE += list(tail_of(B - 1))

    SHARED_STEPS = ("norm1", "query", "maxrows", "normalise", "turn_o", "project", "turn_f", "route", "turn_w", "bias2")
    SETUP_SHARED = 0
    shared_use = {step: n for n, step in enumerate([st for st in SCHEDULE if st[0] in SHARED_STEPS])}

    stack = ExitStack()
    with stack:
        def sb(name, shape, dt=f32):
            return stack.enter_context(nc.sbuf_tensor(name, shape, dt))

        def sem(name):
            return stack.enter_context(nc.semaphore(name))

        xs = sb("xs", [128, NT, D])
        ctxA = sb("ctxA", [KA, B, D])
        ctxB = sb("ctxB", [KR, B, D])
        wq = sb("wq", [D, D])
        wk = sb("wk", [D, D])
        wv = sb("wv", [D, D])
        wo = sb("wo", [D, D])
        wr = sb("wr", [D, E])
        rows = sb("rows", [1, 4 * D + E])
        w1 = sb("w1", [D, NE, C * 128])
        w2 = sb("w2", [128, NE, C, D])
        b1r = sb("b1r", [NE * C, 128])
        b2 = sb("b2", [NE, D])
        ident = sb("ident", [128, 128])
        ones = sb("ones", [1, 128])
        tri = sb("tri", [128, E, E])
        masksel = sb("masksel", [128, 128])
        prow = sb("prow", [1, 2 * SL + 2, 128])
        colsb = sb("colsb", [128, 4 * SL + 2])
        b1c = sb("b1c", [128, NE * C])
        bcur = sb("bcur", [128, C])
        bvB = sb("bvB", [128, D])
        boB = sb("boB", [128, D])
        rbB = sb("rbB", [128, E])
        wqS = sb("wqS", [D, SL, G, R])
        wkS = sb("wkS", [D, SL, G, R])
        wrh = sb("wrh", [D, E], f16)
        wrl = sb("wrl", [D, E], f16)
        w1h = sb("w1h", [D, NE, C * 128], f16)
        w1l = sb("w1l", [D, NE, C * 128], f16)
        w2h = sb("w2h", [128, NE, C, D], f16)
        w2l = sb("w2l", [128, NE, C, D], f16)
        ctxT = sb("ctxT", [D, B, KP])
        ctxT4 = sb("ctxT4", [D, B, G, KR])
        asum = sb("asum", [128, 2, B])
        maskcol = sb("maskcol", [128, 2, B])
        maskmat = sb("maskmat", [128, 2, B, 128])
        maskrows = sb("maskrows", [128, B, KP])
        khalf = sb("khalf", [128, 2, 2, KP], f16)
        krest = sb("krest", [128, 2, 2, KP])
        kall = sb("kall", [128, B, SL, KP], f16)
        kd = sb("kd", [128, B, SL, G, KP], f16)
        kdr = sb("kdr", [128, B, SL, G, KR], f16)
        va = sb("va", [KA, B, H, R])
        vb = sb("vb", [128, B, SL, G, R])
        stats = sb("stats", [128, T, 6])
        meanvar = sb("meanvar", [128, T, 2])
        varp = sb("varp", [128, T])
        rstd = sb("rstd", [128, T])
        powc = sb("powc", [128, T])
        xn = sb("xn", [128, T, D])
        xnT = sb("xnT", [D, L])
        qhalf = sb("qhalf", [128, 2, L], f16)
        qs = sb("qs", [128, 2, SL, L], f16)
        mx = sb("mx", [128, T, SL, G])
        mneg = sb("mneg", [128, T, SL * G])
        maxT = sb("maxT", [SL * G, L], f16)
        pr = sb("pr", [128, PR, L])
        oT = sb("oT", [128, 2, L])
        den = sb("den", [128, T, G])
        rden = sb("rden", [128, T, G])
        o = sb("o", [128, T, SL, G, DH])
        omT = sb("omT", [D, L])
        xb = sb("xb", [128, NT, D])
        stats2 = sb("stats2", [128, T, 6])
        meanvar2 = sb("meanvar2", [128, T, 2])
        varp2 = sb("varp2", [128, T])
        rstd2 = sb("rstd2", [128, T])
        xn2 = sb("xn2", [128, T, D])
        fh = sb("fh", [D, NT * 128], f16)
        fl = sb("fl", [D, NT * 128], f16)
        lg = sb("lg", [128, T, E])
        lmax = sb("lmax", [128, T])
        lsh = sb("lsh", [128, T, E])
        pe_ = sb("pexp", [128, T, E])
        psumr = sb("psumr", [128, T])
        pinv = sb("pinv", [128, T])
        gt = sb("gt", [128, T, E, E])
        eqt = sb("eqt", [128, T, E, E])
        rank = sb("rank", [128, T, E])
        gate = sb("gate", [128, NT, NE])
        gate64 = sb("gate64", [128, NT, NE])
        gateT = sb("gateT", [NE, L])
        h32 = sb("h32", [128, 2, C, L])
        hh = sb("hh", [128, 2, C, L], f16)
        hl = sb("hl", [128, 2, C, L], f16)

        banks = stack.enter_context(nc.psum_tensor("banks", [128, 8, 512], f32))
        MAXB, SCOREB, PVB, SHB = 0, 4, 6, 7
        shared = banks[:, SHB, :]

        ctx_loaded, wkv_loaded, wq_loaded, wo_loaded = sem("ctx_loaded"), sem("wkv_loaded"), sem("wq_loaded"), sem("wo_loaded")
        x_loaded = [sem(f"x_loaded{b}") for b in range(B)]
        small_loaded, ffn_loaded = sem("small_loaded"), sem("ffn_loaded")
        pool_step, act_step, dve_step = sem("pool_step"), sem("act_step"), sem("dve_step")
        padded = sem("padded")
        consts_ready = sem("consts_ready")
        wpad_ready = sem("wpad_ready")
        setup_pe, setup_dve, setup_act = sem("setup_pe"), sem("setup_dve"), sem("setup_act")
        shared_full, x2_ready = sem("shared_full"), sem("x2_ready")
        xb_ready = sem("xb_ready")
        var_ready, rstd_ready = sem("var_ready"), sem("rstd_ready")
        xn_ready, xnT_ready = sem("xn_ready"), sem("xnT_ready")
        qhalf_ready, qs_ready = sem("qhalf_ready"), sem("qs_ready")
        maxp_full, maxp_free = sem("maxp_full"), sem("maxp_free")
        mneg_ready, maxT_ready, maxrow_ready = sem("mneg_ready"), sem("maxT_ready"), sem("maxrow_ready")
        score_full, exp_done, pv_done = sem("score_full"), sem("exp_done"), sem("pv_done")
        oT_ready = sem("oT_ready")
        o_ready, omT_ready = sem("o_ready"), sem("omT_ready")
        xn2_ready, fh_ready, fl_ready = sem("xn2_ready"), sem("fh_ready"), sem("fl_ready")
        lsh_ready, pexp_ready, gate_ready, gateT_ready, acc_ready = (
            sem("lsh_ready"), sem("pexp_ready"), sem("gate_ready"), sem("gateT_ready"), sem("acc_ready"))
        w64_ready, w_hi_ready, w_lo_ready = sem("w64_ready"), sem("w_hi_ready"), sem("w_lo_ready")
        up_full, gelu_done, hh_ready, hl_ready = sem("up_full"), sem("gelu_done"), sem("hh_ready"), sem("hl_ready")
        down_full, down_free = sem("down_full"), sem("down_free")
        stored, bias_taken = sem("stored"), sem("bias_taken")

        block = stack.enter_context(nc.Block())

        x_v = x.rearrange("b (t p) d -> p (b t) d", p=128)
        out_v = out.rearrange("b (t p) d -> p (b t) d", p=128)

        @block.sync
        def _(sp):
            sp.dma_start(ctxA[:, :, :], ctx_in[:, 0:KA, :].rearrange("b k d -> k b d")).then_inc(ctx_loaded, 16)
            sp.wait_ge(padded, 1)
            sp.dma_start(ctxB[0:KB, :, :], ctx_in[:, KA:KEYS, :].rearrange("b k d -> k b d")).then_inc(ctx_loaded, 16)
            sp.dma_start(xs[:, 0:T, :], x_v[:, 0:T, :]).then_inc(x_loaded[0], 16)
            sp.dma_start(wk[:, :], Wk).then_inc(wkv_loaded, 16)
            sp.dma_start(wv[:, :], Wv).then_inc(wkv_loaded, 16)
            for b in range(1, B):
                sp.dma_start(xs[:, b * T:(b + 1) * T, :], x_v[:, b * T:(b + 1) * T, :]).then_inc(x_loaded[b], 16)
            sp.dma_start(w1[:, 1:NE, :], rw1.rearrange("e d h -> d e h")).then_inc(ffn_loaded, 16)
            sp.dma_start(w1[:, 0, :], sw1).then_inc(ffn_loaded, 16)
            sp.dma_start(w2[:, 1:NE, :, :], rw2.rearrange("e (c p) d -> p e c d", p=128)).then_inc(ffn_loaded, 16)
            sp.dma_start(w2[:, 0, :, :], sw2.rearrange("(c p) d -> p c d", p=128)).then_inc(ffn_loaded, 16)
            for b in range(B):
                sp.wait_ge(maxT_ready, b + 1)
                for s in range(SL):
                    sp.dma_start(qs[MAXROW:128:R, b % 2, s, :], maxT[G * s:G * s + G, :]).then_inc(maxrow_ready, 16)
            last = (NE - 1) * B
            for g in range(B):
                sp.wait_ge(down_free, last + g + 1)
                sp.dma_start(out_v[:, g * T:(g + 1) * T, :], xb[:, g * T:(g + 1) * T, :]).then_inc(stored, 16)
            sp.wait_ge(stored, 16 * B)

        @block.gpsimd
        def _(pool):
            steps = [0]

            def after(ins):
                steps[0] += 1
                ins.then_inc(pool_step, 1)
                pool.wait_ge(pool_step, steps[0])

            pool.memset(ctxB[:, :, :], 0.0).then_inc(padded, 1)
            pool.memset(masksel[:, :], 0.0)
            pool.memset(prow[:, :, :], 0.0)
            pool.memset(wkS[:, :, :, :], 0.0)
            pool.memset(wqS[:, :, :, :], 0.0)
            pool.memset(ones[:, :], 1.0)
            after(pool.memset(ident[:, :], 0.0))
            pool.affine_select(out=ident[:, :], in_=ident[:, :], compare_op=ALU.not_equal, fill=1.0, base=0,
                               pattern=[[-1, 128]], channel_multiplier=1)
            pool.memset(masksel[:, MASKROW:128:R], 1.0)
            pool.memset(prow[:, 0:SL, MASKROW:128:R], BIG)
            pool.memset(prow[:, SL:2 * SL, MAXROW:128:R], MAXUNIT)
            low = prow[:, 2 * SL:2 * SL + 2, :].rearrange("o a (g r) -> o a g r", r=R)
            pool.memset(low[:, 0, :, DH:2 * DH], 1.0)
            after(pool.memset(low[:, 1, :, 2 * DH:3 * DH], 1.0))
            pool.wait_ge(small_loaded, 16 * 5)
            for k in range(2):
                brow = rows[:, k * D:(k + 1) * D].rearrange("o (s g d) -> o s g d", g=G, d=DH)
                brow_pad = prow[:, k * SL:(k + 1) * SL, :].rearrange("o s (g r) -> o s g r", r=R)
                for part in range(3):
                    last = pool.tensor_copy(brow_pad[:, :, :, part * DH:(part + 1) * DH], brow)
            last.then_inc(consts_ready, 1)
            pool.wait_ge(wkv_loaded, 32)
            for part in range(3):
                last = pool.tensor_copy(wkS[:, :, :, part * DH:(part + 1) * DH],
                                        wk[:, :].rearrange("p (s g d) -> p s g d", g=G, d=DH))
            last.then_inc(wpad_ready, 1)
            pool.wait_ge(wq_loaded, 16)
            for part in range(3):
                last = pool.tensor_copy(wqS[:, :, :, part * DH:(part + 1) * DH],
                                        wq[:, :].rearrange("p (s g d) -> p s g d", g=G, d=DH))
            last.then_inc(wpad_ready, 1)

            def rsqrt(n, v, r):
                pool.wait_ge(var_ready, n)
                pool.tensor_tensor(r[:, :], v[:, :], powc[:, :], ALU.pow).then_inc(rstd_ready, 1)

            norms = [(name, b) for name, b, _ in SCHEDULE if name in ("norm1", "norm2")]

            def norm(n):
                name, b = norms[n]
                rsqrt(n + 1, varp if name == "norm1" else varp2, rstd if name == "norm1" else rstd2)

            pool.memset(va[:, :, :, :], 0.0)
            after(pool.memset(vb[:, :, :, :, :], 0.0))
            after(pool.memset(va[:, :, :, DH:DH + 1], 1.0))
            for g in range(G):
                after(pool.memset(vb[g * R:(g + 1) * R, :, :, g, DH:DH + 1], 1.0))
            pool.memset(powc[:, :], -0.5).then_inc(wpad_ready, 1)
            norm(0)
            norm(1)
            pool.memset(gate[:, :, 0:1], 1.0)
            pool.memset(gate64[:, :, 0:1], 1.0 / WSCALE)
            after(pool.memset(tri[:, :, :], 0.0))
            pool.affine_select(out=tri[:, :, :], in_=tri[:, :, :], compare_op=ALU.is_ge, fill=1.0, base=0,
                               pattern=[[-1, E], [1, E]], channel_multiplier=0).then_inc(wpad_ready, 1)
            pool.wait_ge(setup_dve, 2)
            for b in range(B):
                pool.wait_ge(x_loaded[b], 16)
                for t in range(b * T, (b + 1) * T):
                    last = pool.tensor_tensor(xb[:, t, :], xs[:, t, :], boB[:, :], ALU.add)
                last.then_inc(xb_ready, 1)
            norm(2)
            norm(3)
            pool.wait_ge(w_hi_ready, 1)
            pool.tensor_tensor(w1l[:, :, :], w1[:, :, :], w1h[:, :, :], ALU.subtract).then_inc(w_lo_ready, 1)
            norm(4)
            norm(5)
            pool.wait_ge(w_hi_ready, 2)
            pool.tensor_tensor(w2l[:, :, :, :], w2[:, :, :, :], w2h[:, :, :, :], ALU.subtract).then_inc(w_lo_ready, 1)
            for n in range(6, len(norms)):
                norm(n)

        @block.scalar
        def _(act):
            act.dma_start(rows[:, 0:D], bq.rearrange("(o n) -> o n", o=1)).then_inc(small_loaded, 16)
            act.dma_start(rows[:, D:2 * D], bk.rearrange("(o n) -> o n", o=1)).then_inc(small_loaded, 16)
            act.dma_start(rows[:, 2 * D:3 * D], bv.rearrange("(o n) -> o n", o=1)).then_inc(small_loaded, 16)
            act.dma_start(rows[:, 3 * D:4 * D], bo.rearrange("(o n) -> o n", o=1)).then_inc(small_loaded, 16)
            act.dma_start(rows[:, 4 * D:4 * D + E], router_b.rearrange("(o n) -> o n", o=1)).then_inc(small_loaded, 16)
            act.dma_start(wq[:, :], Wq).then_inc(wq_loaded, 16)
            act.dma_start(wo[:, :], Wo).then_inc(wo_loaded, 16)
            act.dma_start(wr[:, :], router_w).then_inc(wo_loaded, 16)
            act.dma_start(b1r[0:C, :], sb1.rearrange("(c p) -> c p", p=128)).then_inc(wo_loaded, 16)
            act.dma_start(b1r[C:NE * C, :], rb1.rearrange("e (c p) -> (e c) p", p=128)).then_inc(wo_loaded, 16)
            act.dma_start(b2[0:1, :], sb2.rearrange("(o n) -> o n", o=1)).then_inc(wo_loaded, 16)
            act.dma_start(b2[1:NE, :], rb2).then_inc(wo_loaded, 16)

            mK = colsb[:, 2 * SL + 1:2 * SL + 2]
            mQ = colsb[:, 2 * SL:2 * SL + 1]
            act.wait_ge(setup_dve, 1)
            for n in range(2 * SL):
                s, pair = n // 2, n % 2
                act.wait_ge(setup_pe, 3 + n)
                if n >= 2:
                    act.wait_ge(setup_dve, n + 1)
                act.activation(khalf[:, n % 2, :, :], banks[:, MAXB + n % 4, 0:2 * KP].rearrange("p (b k) -> p b k", b=2),
                               ACT.Identity, scale=mK, bias=colsb[:, 3 * SL + 2 + s:3 * SL + 3 + s]).then_inc(setup_act, 1)

            def shared_read(step):
                act.wait_ge(shared_full, shared_use[step] + 1)

            prev = None
            units = 0
            weights = 0
            for step in SCHEDULE:
                name, b, i = step
                if name == "norm1":
                    shared_read(step)
                    if b > 0:
                        act.wait_ge(qs_ready, SL * b)
                    act.activation(xnT[:, :], shared, ACT.Copy).then_inc(xnT_ready, 1)
                elif name == "query":
                    n = b * SL + i
                    shared_read(step)
                    if n >= 2:
                        act.wait_ge(qs_ready, n - 1)
                    act.activation(qhalf[:, n % 2, :], shared, ACT.Identity, scale=mQ,
                                   bias=colsb[:, 2 * SL + 2 + i:2 * SL + 3 + i]).then_inc(qhalf_ready, 1)
                elif name == "maxrows":
                    shared_read(step)
                    if b > 0:
                        act.wait_ge(maxrow_ready, 16 * SL * b)
                    act.activation(maxT[:, :], shared[0:SL * G, :], ACT.Copy).then_inc(maxT_ready, 1)
                elif name in ("scores", "last_pv"):
                    if name == "scores":
                        k = b * UNITS + i
                        act.wait_ge(score_full, k + 1)
                        if k >= PR:
                            act.wait_ge(pv_done, k - PR + 1)
                        act.activation(pr[:, k % PR, :], banks[:, SCOREB + k % 2, :], ACT.Exp, scale=SCALE).then_inc(exp_done, 1)
                        done = k
                    else:
                        done = B * UNITS
                    if done > 0 and done % (G + 1) == 0:
                        n = done // (G + 1) - 1
                        act.wait_ge(pv_done, (n + 1) * (G + 1))
                        if n >= 2:
                            act.wait_ge(o_ready, n - 1)
                        act.activation(oT[:, n % 2, :], banks[:, PVB, :], ACT.Copy).then_inc(oT_ready, 1)
                    if weights < 2 and name == "scores" and b == 1 and i % 5 == 4:
                        w, wh = ((w1, w1h), (w2, w2h))[weights]
                        if weights == 0:
                            act.wait_ge(ffn_loaded, 16 * 4)
                        weights += 1
                        act.activation(w[:], w[:], ACT.Copy, scale=WSCALE).then_inc(w64_ready, 1)
                        act.wait_ge(w64_ready, weights)
                        act.activation(wh[:], w[:], ACT.Copy).then_inc(w_hi_ready, 1)
                elif name == "turn_o":
                    shared_read(step)
                    act.activation(omT[:, :], shared, ACT.Copy).then_inc(omT_ready, 1)
                elif name == "turn_f":
                    shared_read(step)
                    act.activation(fh[:, b * L:(b + 1) * L], shared, ACT.Copy).then_inc(fh_ready, 1)
                elif name == "route":
                    act.wait_ge(lsh_ready, b + 1)
                    act.activation(pe_[:, :, :], lsh[:, :, :], ACT.Exp).then_inc(pexp_ready, 1)
                elif name == "turn_w":
                    shared_read(step)
                    if b > 0:
                        act.wait_ge(acc_ready, b)
                    act.activation(gateT[:, :], shared[0:NE, :], ACT.Copy).then_inc(gateT_ready, 1)

            def take_bias(pos):
                nc.scalar.activation(bcur[:, :], b1c[:, bass.ds(pos * C, C)], ACT.Copy).then_inc(bias_taken, 1)

            def gelu(pos, g, waits=True):
                for c in range(C):
                    act.wait_ge(up_full, (pos * B + g) * C + c + 1)
                    if c == 0 and waits:
                        act.wait_ge(hl_ready, pos * B + g - 1)
                    nc.scalar.activation(h32[:, g % 2, c, :], banks[:, 2 * (g % 2) + c, :], ACT.Gelu, scale=1.0 / WSCALE,
                                         bias=bcur[:, c:c + 1]).then_inc(gelu_done, 1)
                act.wait_ge(gelu_done, (pos * B + g) * C + C)
                if waits:
                    act.wait_ge(down_full, pos * B + g - 1)
                nc.scalar.activation(hh[:, g % 2, :, :], h32[:, g % 2, :, :], ACT.Copy).then_inc(hh_ready, 1)

            take_bias(0)
            act.wait_ge(bias_taken, 1)
            for g in range(B):
                gelu(0, g, waits=g >= 2)
            with act.Fori(1, NE) as pos:
                take_bias(pos)
                act.wait_ge(bias_taken, pos + 1)
                for g in range(B):
                    gelu(pos, g)

        @block.vector
        def _(dve):
            steps = [0]

            def after(ins):
                steps[0] += 1
                ins.then_inc(dve_step, 1)
                dve.wait_ge(dve_step, steps[0])

            mQ = colsb[:, 2 * SL:2 * SL + 1]
            mK = colsb[:, 2 * SL + 1:2 * SL + 2]
            nc.vector.memset(asum[:, :, :], 0.0)
            nc.vector.memset(kd[:, :, :, :, :].bitcast(f32), 0.0)
            nc.vector.memset(kdr[:, :, :, :, :].bitcast(f32), 0.0)
            dve.wait_ge(ctx_loaded, 32)
            nc.vector.memset(colsb[:, :], 0.0)
            after(nc.vector.memset(maskcol[:, :, :], 0.0))
            nc.vector.tensor_reduce(asum[:, 0, :], ctxA[:, :, :], axis=AX.X, op=ALU.add, apply_absolute_value=True)
            after(nc.vector.tensor_reduce(asum[0:KR, 1, :], ctxB[:, :, :], axis=AX.X, op=ALU.add, apply_absolute_value=True))
            after(nc.vector.tensor_scalar(maskcol[:, :, :], asum[:, :, :], THRESHOLD, -BIG, ALU.is_le, ALU.mult))
            dve.wait_ge(consts_ready, 1)
            for b in range(B):
                nc.vector.tensor_scalar(maskmat[:, 0, b, :], masksel[:, :], maskcol[:, 0, b:b + 1], None, ALU.mult)
                last = nc.vector.tensor_scalar(maskmat[0:KR, 1, b, :], masksel[0:KR, :], maskcol[0:KR, 1, b:b + 1], None, ALU.mult)
            after(last)
            dve.wait_ge(setup_pe, 1)
            nc.vector.tensor_copy(ctxT[:, :, 0:KA], banks[:, 4, :].rearrange("p (b k) -> p b k", b=B))
            ctxB_T = banks[:, 5, 0:B * KR].rearrange("p (b k) -> p b k", b=B)
            nc.vector.tensor_copy(ctxT[:, :, KA:KP], ctxB_T)
            for g in range(G):
                nc.vector.tensor_copy(ctxT4[:, :, g, :], ctxB_T)
            after(nc.vector.tensor_copy(colsb[:, 0:2 * SL + 2], banks[:, 6, 0:2 * SL + 2]))
            nc.vector.tensor_scalar(colsb[:, 2 * SL + 2:3 * SL + 2], colsb[:, 0:SL], mQ, None, ALU.mult)
            nc.vector.tensor_scalar(colsb[:, 3 * SL + 2:4 * SL + 2], colsb[:, SL:2 * SL], mK, None, ALU.mult).then_inc(setup_dve, 1)
            dve.wait_ge(setup_pe, 2)
            nc.vector.tensor_copy(bvB[:, :], banks[:, 7, 0:D])
            nc.vector.tensor_copy(rbB[:, :], banks[:, 7, 2 * D:2 * D + E])
            nc.vector.tensor_copy(boB[:, :], banks[:, 7, D:2 * D])
            for pair in range(2):
                last = nc.vector.tensor_copy(maskrows[:, 2 * pair:2 * pair + 2, :],
                                             banks[:, 5 + pair, 0:2 * KP].rearrange("p (b k) -> p b k", b=2))
            last.then_inc(setup_dve, 1)
            dve.wait_ge(setup_dve, 2)
            for n in range(2 * SL):
                s, pair = n // 2, n % 2
                dve.wait_ge(setup_act, n + 1)
                after(nc.vector.scalar_tensor_tensor(krest[:, n % 2, :, :], maskrows[:, 2 * pair:2 * pair + 2, :],
                                                     colsb[:, SL + s:SL + s + 1], khalf[:, n % 2, :, :], ALU.add, ALU.subtract))
                nc.vector.tensor_tensor(kall[:, 2 * pair:2 * pair + 2, s, :],
                                        banks[:, MAXB + n % 4, 0:2 * KP].rearrange("p (b k) -> p b k", b=2),
                                        krest[:, n % 2, :, :], ALU.add).then_inc(setup_dve, 1)
            dve.wait_ge(setup_dve, 2 + 2 * SL)
            for g in range(G):
                nc.vector.tensor_copy(kdr[g * R:(g + 1) * R, :, :, g, :], kall[g * R:(g + 1) * R, :, :, KA:KP])
                nc.vector.tensor_copy(kd[g * R:(g + 1) * R, :, :, g, :], kall[g * R:(g + 1) * R, :, :, :]).then_inc(setup_dve, 1)
            dve.wait_ge(setup_pe, 3 + 2 * SL)
            dve.wait_ge(wpad_ready, 3)
            for b in range(B):
                nc.vector.tensor_tensor(va[:, b, :, 0:DH], banks[:, 4, b * D:(b + 1) * D].rearrange("p (h d) -> p h d", d=DH),
                                        bvB[:, :].rearrange("p (h d) -> p h d", d=DH), ALU.add)
            for g in range(G):
                part = slice(g * R, (g + 1) * R)
                for b in range(B):
                    last = nc.vector.tensor_tensor(
                        vb[part, b, :, g, 0:DH],
                        banks[part, 5, b * D:(b + 1) * D].rearrange("p (s g d) -> p s g d", g=G, d=DH)[:, :, g, :],
                        bvB[part, :].rearrange("p (s g d) -> p s g d", g=G, d=DH)[:, :, g, :], ALU.add)
            last.then_inc(setup_dve, 1)
            dve.wait_ge(wo_loaded, 16 * 6)
            after(nc.vector.tensor_scalar(wr[:, :], wr[:, :], WSCALE, None, ALU.mult))
            after(nc.vector.tensor_copy(wrh[:, :], wr[:, :]))
            nc.vector.tensor_tensor(wrl[:, :], wr[:, :], wrh[:, :], ALU.subtract).then_inc(setup_dve, 1)
            dve.wait_ge(setup_pe, 4 + 2 * SL)
            nc.vector.tensor_copy(b1c[:, :], banks[:, 6, 0:NE * C]).then_inc(setup_dve, 1)

            norms = {(name, b): n for n, (name, b) in enumerate((nm, bb) for nm, bb, _ in SCHEDULE if nm in ("norm1", "norm2"))}

            def layernorm(name, b, rows_in, stats, meanvar, varp, rstd, xn):
                for t in range(T):
                    last = nc.vector.bn_stats(stats[:, t, :], rows_in[:, b * T + t, :])
                after(last)
                for t in range(T):
                    last = nc.vector.bn_aggr(meanvar[:, t, :], stats[:, t, :])
                after(last)
                nc.vector.tensor_scalar(varp[:, :], meanvar[:, :, 1], EPS, None, ALU.add).then_inc(var_ready, 1)
                dve.wait_ge(rstd_ready, norms[(name, b)] + 1)
                for t in range(T):
                    last = nc.vector.tensor_scalar(xn[:, t, :], rows_in[:, b * T + t, :], meanvar[:, t, 0:1],
                                                   rstd[:, t:t + 1], ALU.subtract, ALU.mult)
                return last

            def shared_read(step):
                dve.wait_ge(shared_full, shared_use[step] + 1)

            for step in SCHEDULE:
                name, b, i = step
                if name == "norm1":
                    dve.wait_ge(x_loaded[b], 16)
                    if b > 0:
                        dve.wait_ge(xnT_ready, b)
                    layernorm(name, b, xs, stats, meanvar, varp, rstd, xn).then_inc(xn_ready, 1)
                elif name == "query":
                    n = b * SL + i
                    dve.wait_ge(qhalf_ready, n + 1)
                    if b >= 2:
                        dve.wait_ge(score_full, (b - 1) * UNITS)
                    nc.vector.scalar_tensor_tensor(qs[:, b % 2, i, :], shared, colsb[:, i:i + 1], qhalf[:, n % 2, :],
                                                   ALU.add, ALU.subtract).then_inc(qs_ready, 1)
                elif name == "maxima":
                    n = b * T * SL + i
                    t, s = i // SL, i % SL
                    dve.wait_ge(maxp_full, n + 1)
                    pair = banks[:, MAXB + 2 * (n % 2):MAXB + 2 * (n % 2) + 2, 0:2 * KEYS]
                    nc.vector.tensor_reduce(mx[:, t, s, :], pair.rearrange("p c (g k) -> p c g k", k=KEYS),
                                            axis=AX.X, op=ALU.max).then_inc(maxp_free, 1)
                elif name == "maxrows":
                    dve.wait_ge(maxp_free, (b + 1) * T * SL)
                    if b > 0:
                        dve.wait_ge(maxT_ready, b)
                    nc.vector.tensor_scalar(mneg[:, :, :], mx[:, :, :, :].rearrange("p t s g -> p t (s g)"),
                                            MAXFLOOR, -1.0 / MAXUNIT, ALU.max, ALU.mult).then_inc(mneg_ready, 1)
                elif name == "normalise":
                    shared_read(step)
                    turned = shared.rearrange("p (t g r) -> p t g r", g=G, r=R)
                    if i == 0 and b > 0:
                        dve.wait_ge(omT_ready, b)
                    after(nc.vector.tensor_scalar(den[:, :, :], turned[:, :, :, DH], 1e-30, None, ALU.max))
                    after(nc.vector.reciprocal(rden[:, :, :], den[:, :, :]))
                    nc.vector.tensor_tensor(o[:, :, i, :, :], turned[:, :, :, 0:DH],
                                            rden[:, :, :].unsqueeze(3).broadcast_to([128, T, G, DH]), ALU.mult).then_inc(o_ready, 1)
                elif name == "project":
                    shared_read(step)
                    dve.wait_ge(xb_ready, b + 1)
                    xr = xb[:, b * T:(b + 1) * T, :]
                    nc.vector.tensor_tensor(xr, shared.rearrange("p (t d) -> p t d", d=D), xr, ALU.add).then_inc(x2_ready, 1)
                elif name == "norm2":
                    dve.wait_ge(x2_ready, b + 1)
                    if b > 0:
                        dve.wait_ge(fh_ready, b)
                    layernorm(name, b, xb, stats2, meanvar2, varp2, rstd2, xn2).then_inc(xn2_ready, 1)
                elif name == "turn_f":
                    dve.wait_ge(fh_ready, b + 1)
                    nc.vector.tensor_tensor(fl[:, b * L:(b + 1) * L], shared, fh[:, b * L:(b + 1) * L], ALU.subtract).then_inc(fl_ready, 1)
                elif name == "route":
                    shared_read(step)
                    after(nc.vector.scalar_tensor_tensor(
                        lg[:, :, :], shared[:, 0:T * E].rearrange("p (t e) -> p t e", e=E), 1.0 / WSCALE,
                        rbB[:, :].unsqueeze(1).broadcast_to([128, T, E]), ALU.mult, ALU.add))
                    after(nc.vector.tensor_reduce(lmax[:, :], lg[:, :, :], axis=AX.X, op=ALU.max))
                    nc.vector.tensor_tensor(lsh[:, :, :], lg[:, :, :], lmax[:, :].unsqueeze(2).broadcast_to([128, T, E]),
                                            ALU.subtract).then_inc(lsh_ready, 1)
                    dve.wait_ge(pexp_ready, b + 1)
                    p_e = pe_[:, :, :].unsqueeze(3).broadcast_to([128, T, E, E])
                    p_j = pe_[:, :, :].unsqueeze(2).broadcast_to([128, T, E, E])
                    dve.wait_ge(wpad_ready, 4)
                    nc.vector.tensor_tensor(gt[:, :, :, :], p_j, p_e, ALU.is_gt)
                    after(nc.vector.tensor_tensor(eqt[:, :, :, :], p_j, p_e, ALU.is_equal))
                    after(nc.vector.tensor_tensor(eqt[:, :, :, :], eqt[:, :, :, :],
                                                  tri[:, :, :].unsqueeze(1).broadcast_to([128, T, E, E]), ALU.mult))
                    nc.vector.tensor_reduce(psumr[:, :], pe_[:, :, :], axis=AX.X, op=ALU.add)
                    after(nc.vector.tensor_tensor(gt[:, :, :, :], gt[:, :, :, :], eqt[:, :, :, :], ALU.add))
                    nc.vector.reciprocal(pinv[:, :], psumr[:, :])
                    after(nc.vector.tensor_reduce(rank[:, :, :], gt[:, :, :, :], axis=AX.X, op=ALU.add))
                    gb = gate[:, b * T:(b + 1) * T, 1:NE]
                    after(nc.vector.tensor_scalar(rank[:, :, :], rank[:, :, :], 1.5, None, ALU.is_lt))
                    after(nc.vector.tensor_tensor(rank[:, :, :], rank[:, :, :], pe_[:, :, :], ALU.mult))
                    after(nc.vector.tensor_tensor(gb, rank[:, :, :], pinv[:, :].unsqueeze(2).broadcast_to([128, T, E]), ALU.mult))
                    nc.vector.tensor_scalar(gate64[:, b * T:(b + 1) * T, 1:NE], gb, 1.0 / WSCALE, None, ALU.mult).then_inc(gate_ready, 1)
                elif name == "bias2":
                    shared_read(step)
                    xr = xb[:, b * T:(b + 1) * T, :]
                    nc.vector.tensor_tensor(xr, shared.rearrange("p (t d) -> p t d", d=D), xr, ALU.add).then_inc(acc_ready, 1)

            def experts(pos, g, waits=True):
                dve.wait_ge(gelu_done, (pos * B + g) * C + C)
                dve.wait_ge(hh_ready, pos * B + g + 1)
                nc.vector.tensor_tensor(hl[:, g % 2, :, :], h32[:, g % 2, :, :], hh[:, g % 2, :, :], ALU.subtract).then_inc(hl_ready, 1)

            def gated(pos, g):
                dve.wait_ge(down_full, pos * B + g + 1)
                for t in range(T):
                    n = g * T + t
                    last = nc.vector.scalar_tensor_tensor(xb[:, n, :], banks[:, 4 + g % 2, t * D:(t + 1) * D],
                                                          gate64[:, n, bass.ds(pos, 1)], xb[:, n, :], ALU.mult, ALU.add)
                last.then_inc(down_free, 1)

            dve.wait_ge(acc_ready, B)
            experts(0, 0)
            for g in range(1, B):
                experts(0, g)
                gated(0, g - 1)
            with dve.Fori(1, NE) as pos:
                experts(pos, 0)
                gated(pos - 1, B - 1)
                for g in range(1, B):
                    experts(pos, g)
                    gated(pos, g - 1)
            gated(NE - 1, B - 1)

        @block.tensor
        def _(pe):
            mm = nc.tensor.matmul
            pe.wait_ge(consts_ready, 1)
            pe.wait_ge(ctx_loaded, 32)
            for b in range(B):
                nc.tensor.transpose(banks[:, 4, b * KA:(b + 1) * KA], ctxA[:, b, :], ident[:, :])
                nc.tensor.transpose(banks[:, 5, b * KR:(b + 1) * KR], ctxB[:, b, :], ident[0:KR, 0:KR])
            for n in range(2 * SL + 2):
                last = mm(banks[:, 6, n:n + 1], prow[0:1, n, :], ones[0:1, 0:1], start=True, stop=True)
            last.then_inc(setup_pe, 1)
            for k, (a, z) in enumerate(((2 * D, 3 * D), (3 * D, 4 * D), (4 * D, 4 * D + E))):
                mm(banks[:, 7, k * D:k * D + z - a], ones[0:1, :], rows[0:1, a:z], start=True, stop=True)
            pe.wait_ge(setup_dve, 1)
            for b in range(B):
                bank, at = 5 + b // 2, (b % 2) * KP
                mm(banks[:, bank, at:at + KA], maskmat[:, 0, b, :], ident[:, :], start=True, stop=True)
                last = mm(banks[:, bank, at + KA:at + KP], maskmat[0:KR, 1, b, :], ident[0:KR, 0:KR], start=True, stop=True)
            last.then_inc(setup_pe, 1)
            pe.wait_ge(wpad_ready, 1)
            for n in range(2 * SL):
                s, pair = n // 2, n % 2
                if n >= 4:
                    pe.wait_ge(setup_dve, 3 + n - 4)
                mm(banks[:, MAXB + n % 4, 0:2 * KP], wkS[:, s, :, :], ctxT[:, 2 * pair:2 * pair + 2, :],
                   start=True, stop=True).then_inc(setup_pe, 1)
            pe.wait_ge(setup_dve, 2)
            for b in range(B):
                mm(banks[:, 4, b * D:(b + 1) * D], ctxT[:, b, 0:KA], wv[:, :], start=True, stop=True)
                last = mm(banks[:, 5, b * D:(b + 1) * D], ctxT4[:, b, :, :], wv[:, :], start=True, stop=True)
            last.then_inc(setup_pe, 1)
            pe.wait_ge(wo_loaded, 16 * 6)
            nc.tensor.transpose(banks[:, 6, 0:NE * C], b1r[:, :], ident[0:NE * C, 0:NE * C]).then_inc(setup_pe, 1)
            pe.wait_ge(setup_dve, 2 + 2 * SL + G + 3)

            readers = {"norm1": xnT_ready, "query": qs_ready, "maxrows": maxT_ready, "normalise": o_ready, "turn_o": omT_ready,
                       "project": x2_ready, "turn_f": fl_ready, "route": lsh_ready, "turn_w": gateT_ready, "bias2": acc_ready}
            reads = {name: 0 for name in readers}
            before = [None]

            def shared_write(step):
                if before[0]:
                    pe.wait_ge(readers[before[0]], reads[before[0]])
                reads[step[0]] += 1
                before[0] = step[0]

            def weighted_sum(k):
                b, s, j = k // UNITS, k % UNITS // (G + 1), k % (G + 1)
                pe.wait_ge(exp_done, k + 1)
                n = k // (G + 1)
                if j == 0:
                    if n > 0:
                        pe.wait_ge(oT_ready, n)
                    mm(banks[:, PVB, :], vb[:, b, s, :, :], pr[:, k % PR, :], start=True, stop=False,
                       skip_group_check=True).then_inc(pv_done, 1)
                else:
                    g = j - 1
                    last = mm(banks[g * R:(g + 1) * R, PVB, :], va[:, b, s * G + g, :], pr[:, k % PR, :],
                              start=False, stop=True, skip_group_check=True)
                    last.then_inc(pv_done, 1)

            for step in SCHEDULE:
                name, b, i = step
                if name == "norm1":
                    shared_write(step)
                    pe.wait_ge(xn_ready, b + 1)
                    for t in range(T):
                        last = nc.tensor.transpose(shared[:, t * 128:(t + 1) * 128], xn[:, t, :], ident[:, :])
                    last.then_inc(shared_full, 1)
                elif name == "query":
                    shared_write(step)
                    if b == 0 and i == 0:
                        pe.wait_ge(wpad_ready, 2)
                    pe.wait_ge(xnT_ready, b + 1)
                    mm(shared, wqS[:, i, :, :], xnT[:, :], start=True, stop=True).then_inc(shared_full, 1)
                elif name == "maxima":
                    n = b * T * SL + i
                    t, s = i // SL, i % SL
                    pe.wait_ge(qs_ready, b * SL + s + 1)
                    if n >= 2:
                        pe.wait_ge(maxp_free, n - 1)
                    for c in range(2):
                        last = mm(banks[:, MAXB + 2 * (n % 2) + c, 0:2 * KEYS], qs[:, b % 2, s, t * 128:(t + 1) * 128],
                                  kd[:, b, s, 2 * c:2 * c + 2, 0:KEYS], start=True, stop=True)
                    last.then_inc(maxp_full, 1)
                elif name == "maxrows":
                    shared_write(step)
                    pe.wait_ge(mneg_ready, b + 1)
                    for t in range(T):
                        last = nc.tensor.transpose(shared[0:SL * G, t * 128:(t + 1) * 128], mneg[:, t, :], ident[:, :])
                    last.then_inc(shared_full, 1)
                elif name == "scores":
                    k = b * UNITS + i
                    s, j = i // (G + 1), i % (G + 1)
                    if i == 0:
                        pe.wait_ge(maxrow_ready, 16 * SL * (b + 1))
                    if k >= 2:
                        pe.wait_ge(exp_done, k - 1)
                    keys = kdr[:, b, s, :, :] if j == 0 else kd[:, b, s, j - 1, 0:KA]
                    mm(banks[:, SCOREB + k % 2, :], keys, qs[:, b % 2, s, :], start=True, stop=True).then_inc(score_full, 1)
                    if k > 0:
                        weighted_sum(k - 1)
                elif name == "last_pv":
                    weighted_sum(B * UNITS - 1)
                elif name == "normalise":
                    shared_write(step)
                    n = b * SL + i
                    pe.wait_ge(oT_ready, n + 1)
                    for t in range(T):
                        last = nc.tensor.transpose(shared[:, t * 128:(t + 1) * 128], oT[:, n % 2, t * 128:(t + 1) * 128], ident[:, :])
                    last.then_inc(shared_full, 1)
                elif name == "turn_o":
                    shared_write(step)
                    pe.wait_ge(o_ready, (b + 1) * SL)
                    for t in range(T):
                        last = nc.tensor.transpose(shared[:, t * 128:(t + 1) * 128], o[:, t, :, :, :], ident[:, :])
                    last.then_inc(shared_full, 1)
                elif name == "project":
                    shared_write(step)
                    pe.wait_ge(omT_ready, b + 1)
                    for t in range(T):
                        last = mm(shared[:, t * 128:(t + 1) * 128], omT[:, t * 128:(t + 1) * 128], wo[:, :], start=True, stop=True)
                    last.then_inc(shared_full, 1)
                elif name == "turn_f":
                    shared_write(step)
                    pe.wait_ge(xn2_ready, b + 1)
                    for t in range(T):
                        last = nc.tensor.transpose(shared[:, t * 128:(t + 1) * 128], xn2[:, t, :], ident[:, :])
                    last.then_inc(shared_full, 1)
                elif name == "route":
                    shared_write(step)
                    pe.wait_ge(fl_ready, b + 1)
                    for t in range(T):
                        at = slice((b * T + t) * 128, (b * T + t + 1) * 128)
                        to = shared[:, t * E:(t + 1) * E]
                        mm(to, fh[:, at], wrh[:, :], start=True, stop=False)
                        mm(to, fh[:, at], wrl[:, :], start=False, stop=False)
                        last = mm(to, fl[:, at], wrh[:, :], start=False, stop=True)
                    last.then_inc(shared_full, 1)
                elif name == "turn_w":
                    shared_write(step)
                    pe.wait_ge(gate_ready, b + 1)
                    for t in range(T):
                        last = nc.tensor.transpose(shared[0:NE, t * 128:(t + 1) * 128], gate[:, b * T + t, :], ident[:, :])
                    last.then_inc(shared_full, 1)
                elif name == "bias2":
                    shared_write(step)
                    pe.wait_ge(gateT_ready, b + 1)
                    for t in range(T):
                        last = mm(shared[:, t * 128:(t + 1) * 128], gateT[:, t * 128:(t + 1) * 128], b2[:, :], start=True, stop=True)
                    last.then_inc(shared_full, 1)

            def up(pos, g):
                for c in range(C):
                    to = banks[:, 2 * (g % 2) + c, :]
                    hi = w1h[:, bass.ds(pos, 1), c * 128:(c + 1) * 128]
                    lo = w1l[:, bass.ds(pos, 1), c * 128:(c + 1) * 128]
                    fhg, flg = fh[:, g * L:(g + 1) * L], fl[:, g * L:(g + 1) * L]
                    mm(to, hi, fhg, start=True, stop=False)
                    mm(to, hi, flg, start=False, stop=False)
                    mm(to, lo, fhg, start=False, stop=True).then_inc(up_full, 1)

            def down(pos, g, waits=True):
                pe.wait_ge(hl_ready, pos * B + g + 1)
                if waits:
                    pe.wait_ge(down_free, pos * B + g - 1)
                for t in range(T):
                    to = banks[:, 4 + g % 2, t * D:(t + 1) * D]
                    at = slice(t * 128, (t + 1) * 128)
                    for c in range(C):
                        hi = w2h[:, bass.ds(pos, 1), c, :]
                        lo = w2l[:, bass.ds(pos, 1), c, :]
                        mm(to, hh[:, g % 2, c, at], hi, start=c == 0, stop=False)
                        mm(to, hh[:, g % 2, c, at], lo, start=False, stop=False)
                        last = mm(to, hl[:, g % 2, c, at], hi, start=False, stop=c == C - 1)
                last.then_inc(down_full, 1)

            pe.wait_ge(w_lo_ready, 2)
            pe.wait_ge(maxp_free, B * T * SL)
            up(0, 0)
            for g in range(1, B):
                up(0, g)
                down(0, g - 1, waits=g >= 3)
            with pe.Fori(1, NE) as pos:
                up(pos, 0)
                down(pos - 1, B - 1)
                for g in range(1, B):
                    up(pos, g)
                    down(pos, g - 1)
            down(NE - 1, B - 1)


_INS = ['x', 'ctx_1024', 'L0_xattn_Wq', 'L0_xattn_bq', 'L0_xattn_Wk', 'L0_xattn_bk', 'L0_xattn_Wv', 'L0_xattn_bv',
        'L0_xattn_Wo', 'L0_xattn_bo', 'L0_ffn_router_w', 'L0_ffn_router_b', 'L0_ffn_sw1', 'L0_ffn_sb1', 'L0_ffn_sw2',
        'L0_ffn_sb2', 'L0_ffn_rw1', 'L0_ffn_rb1', 'L0_ffn_rw2', 'L0_ffn_rb2']


def kernel(**inputs):
    import numpy as np
    import concourse.bacc as bacc
    from concourse import mybir
    from concourse.bass_utils import run_bass_kernel_spmd

    nc = bacc.Bacc("TRN2", target_bir_lowering=False, num_devices=1)
    arrays, args = {}, []
    for name in _INS:
        a = np.ascontiguousarray(inputs[name])
        arrays[f"in_{name}"] = a
        args.append(nc.dram_tensor(f"in_{name}", a.shape, mybir.dt.from_np(a.dtype), kind="ExternalInput").ap())
    result = nc.dram_tensor("out_x", inputs["x"].shape, mybir.dt.float32, kind="ExternalOutput")
    xattn_moe_kernel(nc, *args, result.ap())
    r = run_bass_kernel_spmd(nc, [arrays], core_ids=[0])
    return r.results[0]["out_x"]
```

```python
import concourse.bass as bass
from concourse import mybir
from contextlib import ExitStack


def xattn_moe_kernel(nc: bass.Bass, x, ctx_in, Wq, bq, Wk, bk, Wv, bv, Wo, bo, router_w, router_b,
                     sw1, sb1, sw2, sb2, rw1, rb1, rw2, rb2, out):
    f32 = mybir.dt.float32
    f16 = mybir.dt.float16
    ALU = mybir.AluOpType
    ACT = mybir.ActivationFunctionType
    AX = mybir.AxisListType

    B, L, D = x.shape
    KEYS = ctx_in.shape[1]
    H, DH = 16, 8
    G = 4
    SL = H // G
    R = 32
    MAXROW, MASKROW = 24, 25
    KA = 128
    KR = 32
    KB = KEYS - KA
    KP = KA + KR
    T = L // 128
    NT = B * T
    E = rw1.shape[0]
    NE = E + 1
    C = rw1.shape[2] // 128
    EPS = 1e-5
    BIG = 65504.0
    MAXUNIT = 1024.0
    MAXFLOOR = -6.0e7
    WSCALE = 64.0
    LEAST = 2.0 ** -126
    THRESHOLD = 102.4
    SCALE = float(DH) ** -0.5
    PR = 6
    UNITS = SL * (G + 1)

    LAG = {
        "consts": {"ACT": 0.0},
        "turn_ctxA": {"PE": 0.0, "ACT": 0.3}, "turn_ctxB": {"PE": 0.0, "ACT": 0.3},
        "columns": {"PE": 0.0, "DVE": 0.3},
        "masks": {"DVE": 0.0},
        "maskrows": {"PE": 0.0, "DVE": 0.3},
        "spread": {"PE": 0.0, "DVE": 0.5},
        "keys": {"PE": 0.0, "ACT": 0.3, "DVE": 0.5},
        "valuesA": {"PE": 0.0, "ACT": 0.4}, "valuesB": {"PE": 0.0, "ACT": 0.4},
        "turn_b1": {"PE": 0.0, "DVE": 0.5},
        "stats1": {"DVE": 0.0, "POOL": 0.5}, "norm1": {"PE": 0.0, "ACT": 0.4},
        "query": {"PE": 0.0, "ACT": 0.4, "DVE": 0.8},
        "maxima": {"PE": 0.0, "DVE": 0.4},
        "maxrows": {"DVE": 0.0, "PE": 0.2, "ACT": 0.5, "SP": 0.6},
        "scores": {"PE": 0.0, "ACT": 0.5}, "sums": {"PE": 0.0}, "take_sums": {"ACT": 0.0},
        "normalise": {"PE": 0.0, "DVE": 0.5},
        "turn_o": {"PE": 0.0, "ACT": 0.4},
        "residual": {"POOL": 0.0},
        "project": {"PE": 0.0, "DVE": 0.5},
        "stats2": {"DVE": 0.0, "POOL": 0.5}, "turn_f": {"PE": 0.0, "ACT": 0.4, "DVE": 0.8},
        "route": {"PE": 0.0, "DVE": 0.4, "ACT": 0.8, "POOL": 1.1}, "gates": {"DVE": 0.0},
        "turn_w": {"PE": 0.0, "ACT": 0.4}, "bias2": {"PE": 0.0, "DVE": 0.4},
        "split_w": {"ACT": 0.0}, "low_w": {"POOL": 0.0}, "split_router": {"DVE": 0.0},
        "up": {"PE": 0.0, "ACT": 0.3, "DVE": 0.6}, "down": {"PE": 0.0, "DVE": 0.5},
    }
    HALVES = 2
    steps_at = [(-30, "turn_ctxA", 0, 0), (-29.5, "turn_ctxB", 0, 0), (-29, "consts", 0, 0), (-28, "columns", 0, 0),
                (-31, "masks", 0, 0), (-26, "maskrows", 0, 0), (0.6, "maskrows", 1, 0), (1.7, "spread", 0, 0),
                (-1.3, "valuesA", 0, 0), (-0.6, "valuesB", 0, 0), (17.6, "turn_b1", 0, 0), (16.5, "split_router", 0, 0)]
    steps_at += [(-7.1 + 3.5 * s, "keys", 0, s) for s in range(SL)] + [(7.3 + 3.7 * s, "keys", 1, s) for s in range(SL)]
    steps_at += [(5.0 * b + 3.0, "residual", b, 0) for b in range(B)]
    steps_at += [(30.3, "split_w", 0, 0), (36.3, "split_w", 1, 0)]
    steps_at += [(34.0 + 2.2 * k, "low_w", k // NE, k % NE) for k in range(2 * NE)]
    for b in range(B):
        t0, first = UNITS * b, b == 0
        base = UNITS * (b - 1)
        steps_at.append((-30.0 if first else base + 1.0, "stats1", b, 0))
        steps_at.append((-24.0 if first else base + 4.15, "norm1", b, 0))
        for s in range(SL):
            at = -6.5 + 3.5 * s if first else base + 5.2 + 3.7 * s
            after_query, gap = (1.9, 0.37) if first else (4.0, 0.45)
            steps_at.append((at, "query", b, s))
            steps_at += [(at + after_query + gap * n, "maxima", b, s * T * HALVES + n) for n in range(T * HALVES)]
            steps_at.append((at + after_query + 0.5 + gap * T * HALVES, "maxrows", b, s))
            steps_at.append((t0 + (G + 1) * (s + 1) + 0.9, "take_sums", b, s))
            steps_at.append((t0 + (G + 1) * (s + 1) + 1.9, "normalise", b, s))
        for k in range(UNITS):
            steps_at.append((t0 + k, "scores", b, k))
            steps_at.append((t0 + k + 1.6, "sums", b, k))
        end = t0 + UNITS
        steps_at += [(end + dt, name, b, 0) for dt, name in (
            (3.4, "turn_o"), (4.6, "project"), (5.2, "stats2"), (8.0, "turn_f"), (9.5, "route"), (12.5, "gates"),
            (13.5, "turn_w"), (14.7, "bias2"))]
    end = UNITS * B
    steps_at += [(end + 2.2, "up", 0, 0), (end + 3.2, "up", 0, 1), (end + 6.5, "up", 0, 2), (end + 7.0, "down", 0, 0),
                 (end + 12.0, "up", 0, 3), (end + 12.5, "down", 0, 1)]

    def order(engine):
        parts = [(at + LAG[name][engine], n, (name, b, i)) for n, (at, name, b, i) in enumerate(steps_at) if engine in LAG[name]]
        return [step for _, _, step in sorted(parts)]

    SHARED_STEPS = ("turn_ctxA", "turn_ctxB", "columns", "maskrows", "spread", "keys", "valuesA", "valuesB", "turn_b1", "norm1",
                    "query", "maxrows", "normalise", "turn_o", "project", "turn_f", "route", "turn_w", "bias2")
    shared_use = {step: n for n, step in enumerate([st for st in order("PE") if st[0] in SHARED_STEPS])}

    stack = ExitStack()
    with stack:
        def sb(name, shape, dt=f32):
            return stack.enter_context(nc.sbuf_tensor(name, shape, dt))

        def sem(name):
            return stack.enter_context(nc.semaphore(name))

        xs = sb("xs", [128, NT, D])
        ctxA = sb("ctxA", [KA, B, D])
        ctxB = sb("ctxB", [KR, B, D])
        wq = sb("wq", [D, D])
        wk = sb("wk", [D, D])
        wv = sb("wv", [D, D])
        wo = sb("wo", [D, D])
        wr = sb("wr", [D, E])
        rows = sb("rows", [1, 4 * D + E])
        w1 = sb("w1", [D, NE, C * 128])
        w2 = sb("w2", [128, NE, C, D])
        b1r = sb("b1r", [NE * C, 128])
        b2 = sb("b2", [NE, D])
        ident = sb("ident", [128, 128])
        ones = sb("ones", [1, 128])
        tri = sb("tri", [128, E, E])
        masksel = sb("masksel", [128, 128])
        powc = sb("powc", [128, T])
        prow = sb("prow", [1, 2 * SL + 2, 128])
        cols = sb("cols", [128, 4 * SL + 2])
        b1c = sb("b1c", [128, NE * C])
        bcur = sb("bcur", [128, C])
        boB = sb("boB", [128, D])
        rbB = sb("rbB", [128, E])
        wqS = sb("wqS", [D, SL, G, R])
        wkS = sb("wkS", [D, SL, G, R])
        wrh = sb("wrh", [D, E], f16)
        wrl = sb("wrl", [D, E], f16)
        w1h = sb("w1h", [D, NE, C * 128], f16)
        w1l = sb("w1l", [D, NE, C * 128], f16)
        w2h = sb("w2h", [128, NE, C, D], f16)
        w2l = sb("w2l", [128, NE, C, D], f16)
        ctxT = sb("ctxT", [D, B, KP])
        ctxT4 = sb("ctxT4", [D, B, G, KR])
        asum = sb("asum", [128, 2, B])
        maskcol = sb("maskcol", [128, 2, B])
        maskmat = sb("maskmat", [128, 2, B, 128])
        maskrows = sb("maskrows", [128, B, KP])
        khalf = sb("khalf", [128, 2, 2, KP], f16)
        krest = sb("krest", [128, 2, KP])
        kall = sb("kall", [128, 2, KP], f16)
        kd = sb("kd", [128, B, SL, G, KP], f16)
        kdr = sb("kdr", [128, B, SL, G, KR], f16)
        va = sb("va", [KA, B, H, R])
        vb = sb("vb", [128, B, SL, G, R])
        stats = sb("stats", [128, T, 6])
        meanvar = sb("meanvar", [128, T, 2])
        varp = sb("varp", [128, T])
        rstd = sb("rstd", [128, T])
        xn = sb("xn", [128, T, D])
        xnT = sb("xnT", [D, L])
        qhalf = sb("qhalf", [128, 2, L], f16)
        qs = sb("qs", [128, 2, SL, L], f16)
        mx = sb("mx", [128, SL, T, G])
        mneg = sb("mneg", [128, 2, T, G])
        maxT = sb("maxT", [G, 2, L], f16)
        pr = sb("pr", [128, PR, L])
        oT = sb("oT", [128, 2, L])
        den = sb("den", [128, T, G])
        rden = sb("rden", [128, T, G])
        o = sb("o", [128, T, SL, G, DH])
        omT = sb("omT", [D, L])
        xb = sb("xb", [128, NT, D])
        stats2 = sb("stats2", [128, T, 6])
        meanvar2 = sb("meanvar2", [128, T, 2])
        varp2 = sb("varp2", [128, T])
        rstd2 = sb("rstd2", [128, T])
        xn2 = sb("xn2", [128, T, D])
        fh = sb("fh", [D, NT * 128], f16)
        fl = sb("fl", [D, NT * 128], f16)
        logits = sb("logits", [128, T, E])
        lmax = sb("lmax", [128, T])
        lsh = sb("lsh", [128, T, E])
        pexp = sb("pexp", [128, T, E])
        psum_e = sb("psum_e", [128, T])
        pinv = sb("pinv", [128, T])
        above = sb("above", [128, T, E, E])
        rank = sb("rank", [128, T, E])
        gate = sb("gate", [128, NT, NE])
        gate64 = sb("gate64", [128, NT, NE])
        gateT = sb("gateT", [NE, L])
        h32 = sb("h32", [128, 2, C, L])
        hh = sb("hh", [128, B, C, L], f16)
        hl = sb("hl", [128, B, C, L], f16)

        banks = stack.enter_context(nc.psum_tensor("banks", [128, 8, 512], f32))
        MAXBANKS, SCOREB, PVB, SHAREDB = 3, 4, 6, (3, 7)
        UPB = (0, 1, 2, 6)
        DOWNB = 4

        def shared(step):
            return banks[:, SHAREDB[shared_use[step] % 2], :]

        ctx_loaded, wkv_loaded, wq_loaded, ffn_loaded = sem("ctx_loaded"), sem("wkv_loaded"), sem("wq_loaded"), sem("ffn_loaded")
        x_loaded = [sem(f"x_loaded{b}") for b in range(B)]
        small_loaded, rest_loaded = sem("small_loaded"), sem("rest_loaded")
        pool_step, dve_step = sem("pool_step"), sem("dve_step")
        pads_zeroed, consts_made, values_padded, tri_made = sem("pads_zeroed"), sem("consts_made"), sem("values_padded"), sem("tri_made")
        weights_padded = sem("weights_padded")
        shared_full = sem("shared_full")
        ctxT_ready, cols_ready, masks_ready, maskrows_ready = sem("ctxT_ready"), sem("cols_ready"), sem("masks_ready"), sem("maskrows_ready")
        spread_ready, khalf_ready, kall_ready, kd_ready = sem("spread_ready"), sem("khalf_ready"), sem("kall_ready"), sem("kd_ready")
        values_ready, b1c_ready, router_split = sem("values_ready"), sem("b1c_ready"), sem("router_split")
        residual_ready = sem("residual_ready")
        var1_ready, xn1_ready, xnT_ready = sem("var1_ready"), sem("xn1_ready"), sem("xnT_ready")
        qhalf_ready, qs_ready = sem("qhalf_ready"), sem("qs_ready")
        max_full, max_taken = sem("max_full"), sem("max_taken")
        mneg_ready, maxT_ready = sem("mneg_ready"), sem("maxT_ready")
        maxrow_sent = [sem("maxrow_sent0"), sem("maxrow_sent1")]
        score_full, exp_done, sums_done, oT_ready = sem("score_full"), sem("exp_done"), sem("sums_done"), sem("oT_ready")
        o_ready, omT_ready, x2_ready = sem("o_ready"), sem("omT_ready"), sem("x2_ready")
        var2_ready, xn2_ready, fh_ready, fl_ready = sem("var2_ready"), sem("xn2_ready"), sem("fh_ready"), sem("fl_ready")
        lsh_ready, pexp_ready, order_ready = sem("lsh_ready"), sem("pexp_ready"), sem("order_ready")
        gate_ready, gateT_ready, acc_ready = sem("gate_ready"), sem("gateT_ready"), sem("acc_ready")
        w64_ready, w_hi_ready, w_lo_ready = sem("w64_ready"), sem("w_hi_ready"), sem("w_lo_ready")
        up_full, gelu_done, hh_ready, hl_ready = sem("up_full"), sem("gelu_done"), sem("hh_ready"), sem("hl_ready")
        down_full, down_free, bias_taken = sem("down_full"), sem("down_free"), sem("bias_taken")
        stored = sem("stored")

        block = stack.enter_context(nc.Block())

        x_v = x.rearrange("b (t p) d -> p (b t) d", p=128)
        out_v = out.rearrange("b (t p) d -> p (b t) d", p=128)

        def row(v):
            return v.rearrange("(o n) -> o n", o=1)

        @block.sync
        def _(sp):
            sp.dma_start(ctxA[:, :, :], ctx_in[:, 0:KA, :].rearrange("b k d -> k b d")).then_inc(ctx_loaded, 16)
            sp.dma_start(xs[:, 0:T, :], x_v[:, 0:T, :]).then_inc(x_loaded[0], 16)
            sp.wait_ge(pads_zeroed, 1)
            sp.dma_start(ctxB[0:KB, :, :], ctx_in[:, KA:KEYS, :].rearrange("b k d -> k b d")).then_inc(ctx_loaded, 16)
            sp.dma_start(wk[:, :], Wk).then_inc(wkv_loaded, 16)
            sp.dma_start(wv[:, :], Wv).then_inc(wkv_loaded, 16)
            for b in range(1, B):
                sp.dma_start(xs[:, b * T:(b + 1) * T, :], x_v[:, b * T:(b + 1) * T, :]).then_inc(x_loaded[b], 16)
            sp.dma_start(w1[:, 1:NE, :], rw1.rearrange("e d h -> d e h")).then_inc(ffn_loaded, 16)
            sp.dma_start(w1[:, 0, :], sw1).then_inc(ffn_loaded, 16)
            sp.dma_start(w2[:, 1:NE, :, :], rw2.rearrange("e (c p) d -> p e c d", p=128)).then_inc(ffn_loaded, 16)
            sp.dma_start(w2[:, 0, :, :], sw2.rearrange("(c p) d -> p c d", p=128)).then_inc(ffn_loaded, 16)
            for name, b, s in order("SP"):
                n = b * SL + s
                sp.wait_ge(maxT_ready, n + 1)
                sp.dma_start(qs[MAXROW:128:R, b % 2, s, :], maxT[:, n % 2, :]).then_inc(maxrow_sent[n % 2], 16)
            last = (NE - 1) * B
            for g in range(B):
                sp.wait_ge(down_free, last + g + 1)
                sp.dma_start(out_v[:, g * T:(g + 1) * T, :], xb[:, g * T:(g + 1) * T, :]).then_inc(stored, 16)
            sp.wait_ge(stored, 16 * B)

        @block.gpsimd
        def _(pool):
            steps = [0]

            def after(ins):
                steps[0] += 1
                ins.then_inc(pool_step, 1)
                pool.wait_ge(pool_step, steps[0])

            pool.memset(ctxB[:, :, :], 0.0).then_inc(pads_zeroed, 1)
            pool.memset(prow[:, :, :], 0.0)
            pool.memset(masksel[:, :], 0.0)
            after(pool.memset(ident[:, :], 0.0))
            pool.affine_select(out=ident[:, :], in_=ident[:, :], compare_op=ALU.not_equal, fill=1.0, base=0,
                               pattern=[[-1, 128]], channel_multiplier=1)
            pool.memset(masksel[:, MASKROW:128:R], 1.0)
            pool.memset(prow[:, 0:SL, MASKROW:128:R], BIG)
            pool.memset(prow[:, SL:2 * SL, MAXROW:128:R], MAXUNIT)
            low = prow[:, 2 * SL:2 * SL + 2, :].rearrange("o a (g r) -> o a g r", r=R)
            pool.memset(low[:, 0, :, DH:2 * DH], 1.0)
            pool.memset(low[:, 1, :, 2 * DH:3 * DH], 1.0)
            pool.memset(wkS[:, :, :, :], 0.0)
            pool.memset(wqS[:, :, :, :], 0.0)
            pool.memset(powc[:, :], -0.5)
            after(pool.memset(ones[:, :], 1.0))
            pool.memset(ones[:, :], 1.0).then_inc(consts_made, 1)

            def rsqrt_norm(n, var_sem, v, r, mv, rows_in, b, to, done):
                pool.wait_ge(var_sem, n)
                after(pool.tensor_tensor(r[:, :], v[:, :], powc[:, :], ALU.pow))
                for t in range(T):
                    last = pool.tensor_scalar(to[:, t, :], rows_in[:, b * T + t, :], mv[:, t, 0:1], r[:, t:t + 1],
                                              ALU.subtract, ALU.mult)
                last.then_inc(done, 1)

            padded = False
            for name, b, i in order("POOL"):
                if name == "stats1":
                    if b > 0:
                        pool.wait_ge(xnT_ready, b)
                    rsqrt_norm(b + 1, var1_ready, varp, rstd, meanvar, xs, b, xn, xn1_ready)
                elif name == "stats2":
                    if b > 0:
                        pool.wait_ge(fh_ready, b)
                    rsqrt_norm(b + 1, var2_ready, varp2, rstd2, meanvar2, xb, b, xn2, xn2_ready)
                elif name == "residual":
                    pool.wait_ge(spread_ready, 1)
                    pool.wait_ge(x_loaded[b], 16)
                    for t in range(b * T, (b + 1) * T):
                        last = pool.tensor_tensor(xb[:, t, :], xs[:, t, :], boB[:, :], ALU.add)
                    last.then_inc(residual_ready, 1)
                elif name == "low_w":
                    w, wh, wl = ((w1, w1h, w1l), (w2, w2h, w2l))[b]
                    pool.wait_ge(w_hi_ready, b + 1)
                    pool.tensor_tensor(wl[:, i], w[:, i], wh[:, i], ALU.subtract).then_inc(w_lo_ready, 1)
                elif name == "route":
                    pool.wait_ge(pexp_ready, b + 1)
                    if b > 0:
                        pool.wait_ge(gate_ready, b)
                    p_e = pexp[:, :, :].unsqueeze(3).broadcast_to([128, T, E, E])
                    p_j = pexp[:, :, :].unsqueeze(2).broadcast_to([128, T, E, E])
                    pool.tensor_tensor(above[:, :, :, :], p_j, p_e, ALU.subtract).then_inc(order_ready, 1)
                if not padded:
                    padded = True
                    pool.memset(va[:, :, :, :], 0.0)
                    after(pool.memset(vb[:, :, :, :, :], 0.0))
                    after(pool.memset(va[:, :, :, DH:DH + 1], 1.0))
                    for g in range(G):
                        after(pool.memset(vb[g * R:(g + 1) * R, :, :, g, DH:DH + 1], 1.0))
                    pool.memset(gate[:, :, 0:1], 1.0)
                    pool.memset(gate64[:, :, 0:1], 1.0 / WSCALE).then_inc(values_padded, 1)
                    after(pool.memset(tri[:, :, :], LEAST))
                    pool.affine_select(out=tri[:, :, :], in_=tri[:, :, :], compare_op=ALU.is_ge, fill=0.0, base=0,
                                       pattern=[[-1, E], [1, E]], channel_multiplier=0).then_inc(tri_made, 1)
                    pool.wait_ge(tri_made, 1)

        @block.scalar
        def _(act):
            for k, v in enumerate((bq, bk, bv, bo)):
                act.dma_start(rows[:, k * D:(k + 1) * D], row(v)).then_inc(small_loaded, 16)
            act.dma_start(rows[:, 4 * D:4 * D + E], row(router_b)).then_inc(small_loaded, 16)
            act.dma_start(wq[:, :], Wq).then_inc(wq_loaded, 16)
            act.dma_start(wo[:, :], Wo).then_inc(rest_loaded, 16)
            act.dma_start(wr[:, :], router_w).then_inc(rest_loaded, 16)
            act.dma_start(b1r[0:C, :], sb1.rearrange("(c p) -> c p", p=128)).then_inc(rest_loaded, 16)
            act.dma_start(b1r[C:NE * C, :], rb1.rearrange("e (c p) -> (e c) p", p=128)).then_inc(rest_loaded, 16)
            act.dma_start(b2[0:1, :], row(sb2)).then_inc(rest_loaded, 16)
            act.dma_start(b2[1:NE, :], rb2).then_inc(rest_loaded, 16)

            lowQ = cols[:, 2 * SL:2 * SL + 1]
            lowK = cols[:, 2 * SL + 1:2 * SL + 2]

            def take_bias(pos):
                nc.scalar.activation(bcur[:, :], b1c[:, bass.ds(pos * C, C)], ACT.Copy).then_inc(bias_taken, 1)

            def gelu(pos, g):
                n = pos * B + g
                for c in range(C):
                    act.wait_ge(up_full, n * C + c + 1)
                    if c == 0 and not (isinstance(pos, int) and n < 2):
                        act.wait_ge(hl_ready, n - 1)
                    nc.scalar.activation(h32[:, g % 2, c, :], banks[:, UPB[2 * (g % 2) + c], :], ACT.Gelu, scale=1.0 / WSCALE,
                                         bias=bcur[:, c:c + 1]).then_inc(gelu_done, 1)
                act.wait_ge(gelu_done, n * C + C)
                if not (isinstance(pos, int) and pos == 0):
                    act.wait_ge(down_full, n - B + 1)
                nc.scalar.activation(hh[:, g, :, :], h32[:, g % 2, :, :], ACT.Copy).then_inc(hh_ready, 1)

            for step in order("ACT"):
                name, b, i = step
                if name in SHARED_STEPS:
                    act.wait_ge(shared_full, shared_use[step] + 1)
                if name == "turn_ctxA":
                    act.activation(ctxT[:, :, 0:KA], shared(step).rearrange("p (b k) -> p b k", b=B), ACT.Copy).then_inc(ctxT_ready, 1)
                elif name == "turn_ctxB":
                    turned = shared(step)[:, 0:B * KR].rearrange("p (b k) -> p b k", b=B)
                    act.activation(ctxT[:, :, KA:KP], turned, ACT.Copy)
                    act.activation(ctxT4[:, :, :, :], turned.unsqueeze(2).broadcast_to([D, B, G, KR]), ACT.Copy).then_inc(ctxT_ready, 1)
                elif name == "consts":
                    act.wait_ge(consts_made, 1)
                    act.wait_ge(small_loaded, 16 * 5)
                    act.wait_ge(wkv_loaded, 32)
                    act.wait_ge(wq_loaded, 16)
                    bias_pad = prow[:, 0:2 * SL, :].rearrange("o s (g r) -> o (s g) r", r=R)
                    for part in range(3):
                        last = act.activation(bias_pad[:, :, part * DH:(part + 1) * DH],
                                              rows[:, 0:2 * D].rearrange("o (h d) -> o h d", d=DH), ACT.Copy)
                    last.then_inc(weights_padded, 1)
                    for w, padded in ((wk, wkS), (wq, wqS)):
                        w_pad = padded[:, :, :, :].rearrange("p s g r -> p (s g) r")
                        for part in range(3):
                            last = act.activation(w_pad[:, :, part * DH:(part + 1) * DH],
                                                  w[:, :].rearrange("p (h d) -> p h d", d=DH), ACT.Copy)
                        last.then_inc(weights_padded, 1)
                elif name == "keys":
                    n = b * SL + i
                    act.wait_ge(cols_ready, 1)
                    if n >= 2:
                        act.wait_ge(kall_ready, n - 1)
                    act.activation(khalf[:, n % 2, :, :], shared(step)[:, 0:2 * KP].rearrange("p (b k) -> p b k", b=2),
                                   ACT.Identity, scale=lowK, bias=cols[:, 3 * SL + 2 + i:3 * SL + 3 + i]).then_inc(khalf_ready, 1)
                elif name == "valuesA":
                    act.wait_ge(values_padded, 1)
                    act.activation(va[:, :, :, :].rearrange("p b h r -> p (b h) r")[:, :, 0:DH],
                                   shared(step).rearrange("p (x d) -> p x d", d=DH), ACT.Copy).then_inc(values_ready, 1)
                elif name == "valuesB":
                    for g in range(G):
                        part = slice(g * R, (g + 1) * R)
                        last = act.activation(vb[part, :, :, :, :].rearrange("p b s g r -> p (b s) g r")[:, :, g, 0:DH],
                                              shared(step)[part, :].rearrange("p (x g d) -> p x g d", g=G, d=DH)[:, :, g, :], ACT.Copy)
                    last.then_inc(values_ready, 1)
                elif name == "norm1":
                    if b > 0:
                        act.wait_ge(shared_full, shared_use["query", b - 1, SL - 1] + 1)
                    act.activation(xnT[:, :], shared(step), ACT.Copy).then_inc(xnT_ready, 1)
                elif name == "query":
                    n = b * SL + i
                    act.wait_ge(cols_ready, 1)
                    if n >= 2:
                        act.wait_ge(qs_ready, n - 1)
                    act.activation(qhalf[:, n % 2, :], shared(step), ACT.Identity, scale=lowQ,
                                   bias=cols[:, 2 * SL + 2 + i:2 * SL + 3 + i]).then_inc(qhalf_ready, 1)
                elif name == "maxrows":
                    n = b * SL + i
                    if n >= 2:
                        act.wait_ge(maxrow_sent[n % 2], 16 * (n // 2))
                    act.activation(maxT[:, n % 2, :], shared(step)[0:G, :], ACT.Copy).then_inc(maxT_ready, 1)
                elif name == "scores":
                    k = b * UNITS + i
                    act.wait_ge(score_full, k + 1)
                    if k >= PR:
                        act.wait_ge(sums_done, k - PR + 1)
                    act.activation(pr[:, k % PR, :], banks[:, SCOREB + k % 2, :], ACT.Exp, scale=SCALE).then_inc(exp_done, 1)
                elif name == "take_sums":
                    n = b * SL + i
                    act.wait_ge(sums_done, (n + 1) * (G + 1))
                    if n >= 2:
                        act.wait_ge(o_ready, n - 1)
                    act.activation(oT[:, n % 2, :], banks[:, PVB, :], ACT.Copy).then_inc(oT_ready, 1)
                elif name == "split_w":
                    w, wh = ((w1, w1h), (w2, w2h))[b]
                    act.wait_ge(ffn_loaded, 16 * 4)
                    act.activation(w[:], w[:], ACT.Copy, scale=WSCALE).then_inc(w64_ready, 1)
                    act.wait_ge(w64_ready, b + 1)
                    act.activation(wh[:], w[:], ACT.Copy).then_inc(w_hi_ready, 1)
                elif name == "turn_o":
                    act.activation(omT[:, :], shared(step), ACT.Copy).then_inc(omT_ready, 1)
                elif name == "turn_f":
                    act.activation(fh[:, b * L:(b + 1) * L], shared(step), ACT.Copy).then_inc(fh_ready, 1)
                elif name == "route":
                    act.wait_ge(lsh_ready, b + 1)
                    act.activation(pexp[:, :, :], lsh[:, :, :], ACT.Exp).then_inc(pexp_ready, 1)
                elif name == "turn_w":
                    if b > 0:
                        act.wait_ge(acc_ready, b)
                    act.activation(gateT[:, :], shared(step)[0:NE, :], ACT.Copy).then_inc(gateT_ready, 1)
                elif name == "up":
                    if i == 0:
                        act.wait_ge(b1c_ready, 1)
                        take_bias(0)
                        act.wait_ge(bias_taken, 1)
                    gelu(0, i)

            take_bias(1)
            act.wait_ge(bias_taken, 2)
            gelu(1, 0)
            gelu(1, 1)
            with act.Fori(1, NE - 1) as pos:
                gelu(pos, 2)
                gelu(pos, 3)
                take_bias(pos + 1)
                act.wait_ge(bias_taken, pos + 2)
                gelu(pos + 1, 0)
                gelu(pos + 1, 1)
            gelu(NE - 1, 2)
            gelu(NE - 1, 3)

        @block.vector
        def _(dve):
            steps = [0]

            def after(ins):
                steps[0] += 1
                ins.then_inc(dve_step, 1)
                dve.wait_ge(dve_step, steps[0])

            def statistics(b, rows_in, stats, meanvar, varp, ready):
                for t in range(T):
                    last = nc.vector.bn_stats(stats[:, t, :], rows_in[:, b * T + t, :])
                after(last)
                for t in range(T):
                    last = nc.vector.bn_aggr(meanvar[:, t, :], stats[:, t, :])
                after(last)
                nc.vector.tensor_scalar(varp[:, :], meanvar[:, :, 1], EPS, None, ALU.add).then_inc(ready, 1)

            def low_parts(pos, g):
                n = pos * B + g
                dve.wait_ge(gelu_done, n * C + C)
                dve.wait_ge(hh_ready, n + 1)
                nc.vector.tensor_tensor(hl[:, g, :, :], h32[:, g % 2, :, :], hh[:, g, :, :], ALU.subtract).then_inc(hl_ready, 1)

            def gated(pos, g):
                dve.wait_ge(down_full, pos * B + g + 1)
                if isinstance(pos, int) and pos == 0:
                    dve.wait_ge(acc_ready, g + 1)
                for t in range(T):
                    n = g * T + t
                    last = nc.vector.scalar_tensor_tensor(xb[:, n, :], banks[:, DOWNB + g % 2, t * D:(t + 1) * D],
                                                          gate64[:, n, bass.ds(pos, 1)], xb[:, n, :], ALU.mult, ALU.add)
                last.then_inc(down_free, 1)

            nc.vector.memset(asum[:, :, :], 0.0)
            nc.vector.memset(cols[:, :], 0.0)
            nc.vector.memset(kd[:, 0:2, :, :, :].bitcast(f32), 0.0)
            after(nc.vector.memset(kdr[:, 0:2, :, :, :].bitcast(f32), 0.0))
            for step in order("DVE"):
                name, b, i = step
                if name in SHARED_STEPS and name != "maxrows":
                    dve.wait_ge(shared_full, shared_use[step] + 1)
                if name == "masks":
                    dve.wait_ge(ctx_loaded, 32)
                    nc.vector.tensor_reduce(asum[:, 0, :], ctxA[:, :, :], axis=AX.X, op=ALU.add, apply_absolute_value=True)
                    after(nc.vector.tensor_reduce(asum[0:KR, 1, :], ctxB[:, :, :], axis=AX.X, op=ALU.add, apply_absolute_value=True))
                    after(nc.vector.tensor_scalar(maskcol[:, :, :], asum[:, :, :], THRESHOLD, -BIG, ALU.is_le, ALU.mult))
                    dve.wait_ge(consts_made, 1)
                    for bb in range(B):
                        nc.vector.tensor_scalar(maskmat[:, 0, bb, :], masksel[:, :], maskcol[:, 0, bb:bb + 1], None, ALU.mult)
                        last = nc.vector.tensor_scalar(maskmat[0:KR, 1, bb, :], masksel[0:KR, :], maskcol[0:KR, 1, bb:bb + 1],
                                                       None, ALU.mult)
                    last.then_inc(masks_ready, 1)
                elif name == "columns":
                    after(nc.vector.tensor_copy(cols[:, 0:2 * SL + 2], shared(step)[:, 0:2 * SL + 2]))
                    nc.vector.tensor_scalar(cols[:, 2 * SL + 2:3 * SL + 2], cols[:, 0:SL], cols[:, 2 * SL:2 * SL + 1], None, ALU.mult)
                    nc.vector.tensor_scalar(cols[:, 3 * SL + 2:4 * SL + 2], cols[:, SL:2 * SL], cols[:, 2 * SL + 1:2 * SL + 2],
                                            None, ALU.mult).then_inc(cols_ready, 1)
                elif name == "maskrows":
                    nc.vector.tensor_copy(maskrows[:, 2 * b:2 * b + 2, :],
                                          shared(step)[:, 0:2 * KP].rearrange("p (b k) -> p b k", b=2)).then_inc(maskrows_ready, 1)
                    if b == 1:
                        nc.vector.memset(kd[:, 2:4, :, :, :].bitcast(f32), 0.0)
                        nc.vector.memset(kdr[:, 2:4, :, :, :].bitcast(f32), 0.0)
                elif name == "spread":
                    nc.vector.tensor_copy(rbB[:, :], shared(step)[:, D:D + E])
                    nc.vector.tensor_copy(boB[:, :], shared(step)[:, 0:D]).then_inc(spread_ready, 1)
                elif name == "keys":
                    n = b * SL + i
                    dve.wait_ge(khalf_ready, n + 1)
                    dve.wait_ge(maskrows_ready, b + 1)
                    after(nc.vector.scalar_tensor_tensor(krest[:, :, :], maskrows[:, 2 * b:2 * b + 2, :], cols[:, SL + i:SL + i + 1],
                                                         khalf[:, n % 2, :, :], ALU.add, ALU.subtract))
                    nc.vector.tensor_tensor(kall[:, :, :], shared(step)[:, 0:2 * KP].rearrange("p (b k) -> p b k", b=2),
                                            krest[:, :, :], ALU.add).then_inc(kall_ready, 1)
                    dve.wait_ge(kall_ready, n + 1)
                    for g in range(G):
                        part = slice(g * R, (g + 1) * R)
                        nc.vector.tensor_copy(kdr[part, 2 * b:2 * b + 2, i, g, :], kall[part, :, KA:KP])
                        last = nc.vector.tensor_copy(kd[part, 2 * b:2 * b + 2, i, g, :], kall[part, :, :])
                    last.then_inc(kd_ready, 1)
                elif name == "turn_b1":
                    nc.vector.tensor_copy(b1c[:, :], shared(step)[:, 0:NE * C]).then_inc(b1c_ready, 1)
                elif name == "split_router":
                    dve.wait_ge(rest_loaded, 16 * 6)
                    after(nc.vector.tensor_scalar(wr[:, :], wr[:, :], WSCALE, None, ALU.mult))
                    after(nc.vector.tensor_copy(wrh[:, :], wr[:, :]))
                    nc.vector.tensor_tensor(wrl[:, :], wr[:, :], wrh[:, :], ALU.subtract).then_inc(router_split, 1)
                elif name == "stats1":
                    dve.wait_ge(x_loaded[b], 16)
                    if b > 0:
                        dve.wait_ge(xn1_ready, b)
                    statistics(b, xs, stats, meanvar, varp, var1_ready)
                elif name == "query":
                    n = b * SL + i
                    dve.wait_ge(qhalf_ready, n + 1)
                    if b >= 2:
                        dve.wait_ge(score_full, (b - 2) * UNITS + (G + 1) * (i + 1))
                    nc.vector.scalar_tensor_tensor(qs[:, b % 2, i, :], shared(step), cols[:, i:i + 1], qhalf[:, n % 2, :],
                                                   ALU.add, ALU.subtract).then_inc(qs_ready, 1)
                elif name == "maxima":
                    n = b * SL * T * HALVES + i
                    s, t, c = i // (T * HALVES), i // HALVES % T, i % HALVES
                    dve.wait_ge(max_full, n + 1)
                    nc.vector.tensor_reduce(mx[:, s, t, 2 * c:2 * c + 2],
                                            banks[:, n % MAXBANKS, 0:2 * KEYS].rearrange("p (g k) -> p g k", k=KEYS),
                                            axis=AX.X, op=ALU.max).then_inc(max_taken, 1)
                elif name == "maxrows":
                    n = b * SL + i
                    dve.wait_ge(max_taken, (n + 1) * T * HALVES)
                    if n >= 2:
                        dve.wait_ge(maxT_ready, n - 1)
                    nc.vector.tensor_scalar(mneg[:, n % 2, :, :], mx[:, i, :, :], MAXFLOOR, -1.0 / MAXUNIT,
                                            ALU.max, ALU.mult).then_inc(mneg_ready, 1)
                elif name == "normalise":
                    turned = shared(step).rearrange("p (t g r) -> p t g r", g=G, r=R)
                    if i == 0 and b > 0:
                        dve.wait_ge(omT_ready, b)
                    after(nc.vector.tensor_scalar(den[:, :, :], turned[:, :, :, DH], 1e-30, None, ALU.max))
                    after(nc.vector.reciprocal(rden[:, :, :], den[:, :, :]))
                    nc.vector.tensor_tensor(o[:, :, i, :, :], turned[:, :, :, 0:DH],
                                            rden[:, :, :].unsqueeze(3).broadcast_to([128, T, G, DH]), ALU.mult).then_inc(o_ready, 1)
                elif name == "project":
                    dve.wait_ge(residual_ready, b + 1)
                    xr = xb[:, b * T:(b + 1) * T, :]
                    nc.vector.tensor_tensor(xr, shared(step).rearrange("p (t d) -> p t d", d=D), xr, ALU.add).then_inc(x2_ready, 1)
                elif name == "stats2":
                    dve.wait_ge(x2_ready, b + 1)
                    if b > 0:
                        dve.wait_ge(xn2_ready, b)
                    statistics(b, xb, stats2, meanvar2, varp2, var2_ready)
                elif name == "turn_f":
                    dve.wait_ge(fh_ready, b + 1)
                    nc.vector.tensor_tensor(fl[:, b * L:(b + 1) * L], shared(step), fh[:, b * L:(b + 1) * L],
                                            ALU.subtract).then_inc(fl_ready, 1)
                elif name == "route":
                    after(nc.vector.scalar_tensor_tensor(
                        logits[:, :, :], shared(step)[:, 0:T * E].rearrange("p (t e) -> p t e", e=E), 1.0 / WSCALE,
                        rbB[:, :].unsqueeze(1).broadcast_to([128, T, E]), ALU.mult, ALU.add))
                    after(nc.vector.tensor_reduce(lmax[:, :], logits[:, :, :], axis=AX.X, op=ALU.max))
                    nc.vector.tensor_tensor(lsh[:, :, :], logits[:, :, :], lmax[:, :].unsqueeze(2).broadcast_to([128, T, E]),
                                            ALU.subtract).then_inc(lsh_ready, 1)
                elif name == "gates":
                    dve.wait_ge(order_ready, b + 1)
                    dve.wait_ge(tri_made, 1)
                    after(nc.vector.tensor_tensor(above[:, :, :, :], above[:, :, :, :],
                                                  tri[:, :, :].unsqueeze(1).broadcast_to([128, T, E, E]), ALU.is_ge))
                    dve.wait_ge(values_padded, 1)
                    nc.vector.tensor_reduce(psum_e[:, :], pexp[:, :, :], axis=AX.X, op=ALU.add)
                    after(nc.vector.tensor_reduce(rank[:, :, :], above[:, :, :, :], axis=AX.X, op=ALU.add))
                    nc.vector.reciprocal(pinv[:, :], psum_e[:, :])
                    after(nc.vector.tensor_scalar(rank[:, :, :], rank[:, :, :], 1.5, None, ALU.is_lt))
                    after(nc.vector.tensor_tensor(rank[:, :, :], rank[:, :, :], pexp[:, :, :], ALU.mult))
                    gb = gate[:, b * T:(b + 1) * T, 1:NE]
                    after(nc.vector.tensor_tensor(gb, rank[:, :, :], pinv[:, :].unsqueeze(2).broadcast_to([128, T, E]), ALU.mult))
                    nc.vector.tensor_scalar(gate64[:, b * T:(b + 1) * T, 1:NE], gb, 1.0 / WSCALE, None, ALU.mult).then_inc(gate_ready, 1)
                elif name == "bias2":
                    xr = xb[:, b * T:(b + 1) * T, :]
                    nc.vector.tensor_tensor(xr, shared(step).rearrange("p (t d) -> p t d", d=D), xr, ALU.add).then_inc(acc_ready, 1)
                elif name == "up":
                    low_parts(0, i)
                elif name == "down":
                    gated(0, i)

            low_parts(1, 0)
            gated(0, 2)
            low_parts(1, 1)
            gated(0, 3)
            with dve.Fori(1, NE - 1) as pos:
                low_parts(pos, 2)
                gated(pos, 0)
                low_parts(pos, 3)
                gated(pos, 1)
                low_parts(pos + 1, 0)
                gated(pos, 2)
                low_parts(pos + 1, 1)
                gated(pos, 3)
            low_parts(NE - 1, 2)
            gated(NE - 1, 0)
            low_parts(NE - 1, 3)
            for g in range(1, B):
                gated(NE - 1, g)

        @block.tensor
        def _(pe):
            mm = nc.tensor.matmul

            read_by = {"turn_ctxA": ctxT_ready, "turn_ctxB": ctxT_ready, "columns": cols_ready, "maskrows": maskrows_ready,
                       "spread": spread_ready, "keys": kall_ready, "valuesA": values_ready, "valuesB": values_ready,
                       "turn_b1": b1c_ready, "norm1": xnT_ready, "query": qs_ready, "maxrows": maxT_ready, "normalise": o_ready,
                       "turn_o": omT_ready, "project": x2_ready, "turn_f": fl_ready, "route": lsh_ready, "turn_w": gateT_ready,
                       "bias2": acc_ready}
            counts = {}
            uses = []

            def turned(step, tiles, ins):
                for t in range(tiles):
                    src = ins(t)
                    width = src.free_size()
                    last = nc.tensor.transpose(shared(step)[0:width, t * 128:(t + 1) * 128], src, ident[:, :])
                last.then_inc(shared_full, 1)

            def up(pos, g):
                for c in range(C):
                    to = banks[:, UPB[2 * (g % 2) + c], :]
                    hi = w1h[:, bass.ds(pos, 1), c * 128:(c + 1) * 128]
                    lo = w1l[:, bass.ds(pos, 1), c * 128:(c + 1) * 128]
                    fhg, flg = fh[:, g * L:(g + 1) * L], fl[:, g * L:(g + 1) * L]
                    mm(to, hi, fhg, start=True, stop=False)
                    mm(to, hi, flg, start=False, stop=False)
                    mm(to, lo, fhg, start=False, stop=True).then_inc(up_full, 1)

            def down(pos, g, more=True):
                n = pos * B + g
                pe.wait_ge(hl_ready, n + 1)
                if not isinstance(pos, int) or n >= 2:
                    pe.wait_ge(down_free, n - 1)
                for t in range(T):
                    to = banks[:, DOWNB + g % 2, t * D:(t + 1) * D]
                    at = slice(t * 128, (t + 1) * 128)
                    if t == T - 1 and more:
                        pe.wait_ge(gelu_done, (n + 1) * C + C)
                    for c in range(C):
                        hi = w2h[:, bass.ds(pos, 1), c, :]
                        lo = w2l[:, bass.ds(pos, 1), c, :]
                        mm(to, hh[:, g, c, at], hi, start=c == 0, stop=False)
                        mm(to, hh[:, g, c, at], lo, start=False, stop=False)
                        last = mm(to, hl[:, g, c, at], hi, start=False, stop=c == C - 1)
                last.then_inc(down_full, 1)

            pe.wait_ge(consts_made, 1)
            for step in order("PE"):
                name, b, i = step
                if name in SHARED_STEPS:
                    n = shared_use[step]
                    if n >= 2:
                        pe.wait_ge(*uses[n - 2])
                    counts[read_by[name]] = counts.get(read_by[name], 0) + 1
                    uses.append((read_by[name], counts[read_by[name]]))
                if name == "turn_ctxA":
                    pe.wait_ge(ctx_loaded, 32)
                    turned(step, B, lambda t: ctxA[:, t, :])
                elif name == "turn_ctxB":
                    for bb in range(B):
                        last = nc.tensor.transpose(shared(step)[:, bb * KR:(bb + 1) * KR], ctxB[:, bb, :], ident[0:KR, 0:KR])
                    last.then_inc(shared_full, 1)
                elif name == "columns":
                    pe.wait_ge(weights_padded, 1)
                    for n in range(2 * SL + 2):
                        last = mm(shared(step)[:, n:n + 1], prow[0:1, n, :], ones[0:1, 0:1], start=True, stop=True)
                    last.then_inc(shared_full, 1)
                elif name == "maskrows":
                    pe.wait_ge(masks_ready, 1)
                    for bb in range(2):
                        to = shared(step)[:, bb * KP:(bb + 1) * KP]
                        mm(to[:, 0:KA], maskmat[:, 0, 2 * b + bb, :], ident[:, :], start=True, stop=True)
                        last = mm(to[:, KA:KP], maskmat[0:KR, 1, 2 * b + bb, :], ident[0:KR, 0:KR], start=True, stop=True)
                    last.then_inc(shared_full, 1)
                elif name == "spread":
                    mm(shared(step)[:, 0:D], ones[0:1, :], rows[0:1, 3 * D:4 * D], start=True, stop=True)
                    mm(shared(step)[:, D:D + E], ones[0:1, :], rows[0:1, 4 * D:4 * D + E], start=True, stop=True).then_inc(shared_full, 1)
                elif name == "keys":
                    pe.wait_ge(weights_padded, 2)
                    pe.wait_ge(ctxT_ready, 2)
                    mm(shared(step)[:, 0:2 * KP], wkS[:, i, :, :], ctxT[:, 2 * b:2 * b + 2, :], start=True, stop=True)\
                        .then_inc(shared_full, 1)
                elif name in ("valuesA", "valuesB"):
                    pe.wait_ge(ctxT_ready, 2)
                    for bb in range(B):
                        keys = ctxT[:, bb, 0:KA] if name == "valuesA" else ctxT4[:, bb, :, :]
                        to = shared(step)[:, bb * D:(bb + 1) * D]
                        mm(to, keys, wv[:, :], start=True, stop=False)
                        last = mm(to, ones[0:1, :], rows[0:1, 2 * D:3 * D], start=False, stop=True)
                    last.then_inc(shared_full, 1)
                elif name == "turn_b1":
                    pe.wait_ge(rest_loaded, 16 * 6)
                    nc.tensor.transpose(shared(step)[:, 0:NE * C], b1r[:, :], ident[0:NE * C, 0:NE * C]).then_inc(shared_full, 1)
                elif name == "norm1":
                    pe.wait_ge(xn1_ready, b + 1)
                    turned(step, T, lambda t: xn[:, t, :])
                elif name == "query":
                    pe.wait_ge(weights_padded, 3)
                    pe.wait_ge(xnT_ready, b + 1)
                    mm(shared(step), wqS[:, i, :, :], xnT[:, :], start=True, stop=True).then_inc(shared_full, 1)
                elif name == "maxima":
                    n = b * SL * T * HALVES + i
                    s, t, c = i // (T * HALVES), i // HALVES % T, i % HALVES
                    pe.wait_ge(qs_ready, b * SL + s + 1)
                    pe.wait_ge(kd_ready, b // 2 * SL + s + 1)
                    if n >= MAXBANKS:
                        pe.wait_ge(max_taken, n - MAXBANKS + 1)
                    mm(banks[:, n % MAXBANKS, 0:2 * KEYS], qs[:, b % 2, s, t * 128:(t + 1) * 128],
                       kd[:, b, s, 2 * c:2 * c + 2, 0:KEYS], start=True, stop=True).then_inc(max_full, 1)
                elif name == "maxrows":
                    n = b * SL + i
                    pe.wait_ge(mneg_ready, n + 1)
                    turned(step, T, lambda t: mneg[:, n % 2, t, :])
                elif name == "scores":
                    k = b * UNITS + i
                    s, j = i // (G + 1), i % (G + 1)
                    n = b * SL + s
                    pe.wait_ge(maxrow_sent[n % 2], 16 * (n // 2 + 1))
                    if k >= 2:
                        pe.wait_ge(exp_done, k - 1)
                    keys = kdr[:, b, s, :, :] if j == 0 else kd[:, b, s, j - 1, 0:KA]
                    mm(banks[:, SCOREB + k % 2, :], keys, qs[:, b % 2, s, :], start=True, stop=True).then_inc(score_full, 1)
                elif name == "sums":
                    k = b * UNITS + i
                    s, j = i // (G + 1), i % (G + 1)
                    n = b * SL + s
                    pe.wait_ge(exp_done, k + 1)
                    if j == 0:
                        if n == 0:
                            pe.wait_ge(values_ready, 2)
                        else:
                            pe.wait_ge(oT_ready, n)
                        mm(banks[:, PVB, :], vb[:, b, s, :, :], pr[:, k % PR, :], start=True, stop=False,
                           skip_group_check=True).then_inc(sums_done, 1)
                    else:
                        g = j - 1
                        mm(banks[g * R:(g + 1) * R, PVB, :], va[:, b, s * G + g, :], pr[:, k % PR, :],
                           start=False, stop=True, skip_group_check=True).then_inc(sums_done, 1)
                elif name == "normalise":
                    n = b * SL + i
                    pe.wait_ge(oT_ready, n + 1)
                    turned(step, T, lambda t: oT[:, n % 2, t * 128:(t + 1) * 128])
                elif name == "turn_o":
                    pe.wait_ge(o_ready, (b + 1) * SL)
                    turned(step, T, lambda t: o[:, t, :, :, :])
                elif name == "project":
                    pe.wait_ge(omT_ready, b + 1)
                    pe.wait_ge(rest_loaded, 16 * 6)
                    for t in range(T):
                        last = mm(shared(step)[:, t * D:(t + 1) * D], omT[:, t * 128:(t + 1) * 128], wo[:, :], start=True, stop=True)
                    last.then_inc(shared_full, 1)
                elif name == "turn_f":
                    pe.wait_ge(xn2_ready, b + 1)
                    turned(step, T, lambda t: xn2[:, t, :])
                elif name == "route":
                    pe.wait_ge(fl_ready, b + 1)
                    pe.wait_ge(router_split, 1)
                    for t in range(T):
                        at = slice((b * T + t) * 128, (b * T + t + 1) * 128)
                        to = shared(step)[:, t * E:(t + 1) * E]
                        mm(to, fh[:, at], wrh[:, :], start=True, stop=False)
                        mm(to, fh[:, at], wrl[:, :], start=False, stop=False)
                        last = mm(to, fl[:, at], wrh[:, :], start=False, stop=True)
                    last.then_inc(shared_full, 1)
                elif name == "turn_w":
                    pe.wait_ge(gate_ready, b + 1)
                    turned(step, T, lambda t: gate[:, b * T + t, :])
                elif name == "bias2":
                    pe.wait_ge(gateT_ready, b + 1)
                    for t in range(T):
                        last = mm(shared(step)[:, t * D:(t + 1) * D], gateT[:, t * 128:(t + 1) * 128], b2[:, :], start=True, stop=True)
                    last.then_inc(shared_full, 1)
                elif name == "up":
                    if i == 0:
                        pe.wait_ge(w_lo_ready, 2 * NE)
                        pe.wait_ge(fl_ready, 1)
                        pe.wait_ge(max_taken, B * SL * T * HALVES)
                    elif i == 1:
                        pe.wait_ge(oT_ready, B * SL)
                    elif i == 2:
                        pe.wait_ge(gelu_done, C)
                    up(0, i)
                elif name == "down":
                    down(0, i)

            up(1, 0)
            down(0, 2)
            up(1, 1)
            down(0, 3)
            with pe.Fori(1, NE - 1) as pos:
                up(pos, 2)
                down(pos, 0)
                up(pos, 3)
                down(pos, 1)
                up(pos + 1, 0)
                down(pos, 2)
                up(pos + 1, 1)
                down(pos, 3)
            up(NE - 1, 2)
            down(NE - 1, 0)
            up(NE - 1, 3)
            down(NE - 1, 1)
            down(NE - 1, 2)
            down(NE - 1, 3, more=False)


_INS = ['x', 'ctx_1024', 'L0_xattn_Wq', 'L0_xattn_bq', 'L0_xattn_Wk', 'L0_xattn_bk', 'L0_xattn_Wv', 'L0_xattn_bv',
        'L0_xattn_Wo', 'L0_xattn_bo', 'L0_ffn_router_w', 'L0_ffn_router_b', 'L0_ffn_sw1', 'L0_ffn_sb1', 'L0_ffn_sw2',
        'L0_ffn_sb2', 'L0_ffn_rw1', 'L0_ffn_rb1', 'L0_ffn_rw2', 'L0_ffn_rb2']


def kernel(**inputs):
    import numpy as np
    import concourse.bacc as bacc
    from concourse import mybir
    from concourse.bass_utils import run_bass_kernel_spmd

    nc = bacc.Bacc("TRN2", target_bir_lowering=False, num_devices=1)
    arrays, args = {}, []
    for name in _INS:
        a = np.ascontiguousarray(inputs[name])
        arrays[f"in_{name}"] = a
        args.append(nc.dram_tensor(f"in_{name}", a.shape, mybir.dt.from_np(a.dtype), kind="ExternalInput").ap())
    result = nc.dram_tensor("out_x", inputs["x"].shape, mybir.dt.float32, kind="ExternalOutput")
    xattn_moe_kernel(nc, *args, result.ap())
    r = run_bass_kernel_spmd(nc, [arrays], core_ids=[0])
    return r.results[0]["out_x"]
```

```python
import concourse.bass as bass
from concourse import mybir
from contextlib import ExitStack


def xattn_moe_kernel(nc: bass.Bass, x, ctx_in, Wq, bq, Wk, bk, Wv, bv, Wo, bo, router_w, router_b,
                     sw1, sb1, sw2, sb2, rw1, rb1, rw2, rb2, out):
    f32 = mybir.dt.float32
    f16 = mybir.dt.float16
    ALU = mybir.AluOpType
    ACT = mybir.ActivationFunctionType
    AX = mybir.AxisListType

    B, L, D = x.shape
    KEYS = ctx_in.shape[1]
    H, DH = 16, 8
    G = 4
    SL = H // G
    R = 32
    MAXROW, MASKROW = 24, 25
    KA = 128
    KR = 32
    KB = KEYS - KA
    KP = KA + KR
    T = L // 128
    NT = B * T
    E = rw1.shape[0]
    NE = E + 1
    C = rw1.shape[2] // 128
    EPS = 1e-5
    BIG = 65504.0
    MAXUNIT = 1024.0
    MAXFLOOR = -6.0e7
    WSCALE = 64.0
    LEAST = 2.0 ** -126
    THRESHOLD = 102.4
    SCALE = float(DH) ** -0.5
    PR = 6
    UNITS = SL * (G + 1)

    LOOPED = 2
    FIRST = [(e, g) for e in range(LOOPED) for g in range(B - 1)] + [(e, B - 1) for e in range(LOOPED)]
    FIRST += [(LOOPED, 0), (LOOPED, 1)]
    EARLY = 2

    LAG = {
        "pad_bias": {"DVE": 0.05}, "pad_weights": {"ACT": 4.58}, "ctx4": {"ACT": 0}, "scale1": {"DVE": 2.04},
        "scale2": {"DVE": 0.88}, "turn_ctxA": {"PE": 0, "ACT": 1.68}, "turn_ctxB": {"PE": 0, "ACT": 4.33},
        "columns": {"PE": 0, "DVE": 0.18}, "masks": {"DVE": 0.21}, "maskrows": {"PE": 0, "DVE": 0},
        "spread": {"PE": 0.15, "DVE": 0.95}, "keys": {"PE": 0.09, "ACT": 0, "DVE": 0.84}, "valuesA": {"PE": 0.22, "ACT": 0},
        "valuesB": {"PE": 0, "ACT": 0.46}, "turn_b1": {"PE": 0.53, "DVE": 0.48}, "stats1": {"DVE": 0, "POOL": 6.77},
        "norm1": {"PE": 0, "ACT": 0}, "query": {"PE": 0, "ACT": 0.62, "DVE": 0.8}, "maxima": {"PE": 0.13, "DVE": 0.4},
        "maxrows": {"DVE": 0, "PE": 0.42, "ACT": 0.5, "SP": 3.21}, "scores": {"PE": 0, "ACT": 0.51}, "sums": {"PE": 0},
        "take_sums": {"ACT": 0.48}, "normalise": {"PE": 0, "DVE": 0.74}, "turn_o": {"PE": 0.22, "ACT": 0},
        "residual": {"POOL": 4.68}, "project": {"PE": 0.18, "DVE": 0}, "stats2": {"DVE": 0, "POOL": 2.33},
        "turn_f": {"PE": 0, "ACT": 0, "DVE": 0.21}, "route": {"PE": 0.29, "DVE": 0.23, "ACT": 0.76, "POOL": 4.99},
        "gates": {"DVE": 0}, "turn_w": {"PE": 0, "ACT": 0}, "bias2": {"PE": 0.43, "DVE": 0.8}, "split_w": {"ACT": 0.57},
        "low_w": {"POOL": 0.09}, "split_router": {"DVE": 0}, "up": {"PE": 0, "ACT": 0, "DVE": 1.14},
        "down": {"PE": 0, "DVE": 0.45},
    }
    HALVES = 2
    ONCE = {
        ("turn_ctxA", 0, 0): -36.68, ("turn_ctxB", 0, 0): -30.55, ("columns", 0, 0): -29.77, ("masks", 0, 0): -32.6,
        ("maskrows", 0, 0): -25.97, ("maskrows", 1, 0): 3.2, ("spread", 0, 0): 0.43, ("valuesA", 0, 0): -0.9,
        ("valuesB", 0, 0): -0.28, ("turn_b1", 0, 0): 20.11, ("split_router", 0, 0): 5.76, ("split_w", 0, 0): 31.5,
        ("split_w", 1, 0): 36.45, ("pad_weights", 0, 0): -29.56, ("pad_bias", 0, 0): -33.19, ("scale1", 0, 0): -33.86,
        ("scale2", 3, 0): 85.66, ("ctx4", 0, 0): -3.18, ("up", 0, 0): 64.9, ("up", 0, 1): 65.14, ("up", 0, 2): 81.24,
        ("up", 0, 3): 86.09, ("up", 0, 4): 87.98, ("up", 0, 5): 89.12, ("up", 0, 6): 98, ("up", 0, 7): 101.33,
        ("up", 0, 8): 103.33, ("up", 0, 9): 103.66, ("down", 0, 0): 66.04, ("down", 0, 1): 70.13, ("down", 0, 2): 87.27,
        ("down", 0, 3): 88.95, ("down", 0, 4): 95.4, ("down", 0, 5): 99.03, ("down", 0, 6): 102.87, ("down", 0, 7): 106.18,
    }
    KEYS_AT = ((-8.72, -4.05, -0.26, 1.78), (8.37, 13.35, 15.41, 20.03))
    QUERY_AT = ((-7.75, -2.9, 1, 3.79),
                (-13.95, -11, -9.01, -1.73),
                (-14.68, -10.97, -5.99, -0.71),
                (-12.63, -12.4, -5.41, -3.82))
    MAXIMA_AT = ((-4.15, -0.71, 3.03, 5.92),
                 (-11.27, -7.21, -3.62, 1.17),
                 (-10.65, -7.22, -3.93, 0.45),
                 (-10.49, -7.09, -3.8, -0.11))
    MAXROWS_AT = ((-0.94, 2.56, 6.34, 11.72),
                  (-6.56, 0.56, 2.49, 7.36),
                  (-5.43, 0.72, 2.69, 6),
                  (-6.81, -0.77, 3.54, 6.1))
    MAXIMA_GAP = (0.35, 0.45, 0.46, 0.45)
    SUMS_AFTER = (1.65, 1.56, 1.9, 1.11)
    REST_AFTER = (1.71, 2.17, 2.29, 2.03)
    TAKE_SUMS_AFTER = (0.54, 0.27, 0.01, -0.3)
    NORMALISE_AFTER = (1.13, 1.54, 1.68, 1.44)
    BATCH_AT = {
        "stats1": (-33, -24.08, -22.44, -23.99),
        "norm1": (-23.52, -15.39, -18.04, -15.19),
        "residual": (-2.8, -10.09, -26.29, -45.12),
        "turn_o": (22.23, 22.38, 24.57, 23.71),
        "project": (24.78, 23.01, 24.77, 24.39),
        "stats2": (26.12, 26.79, 24.88, 25.7),
        "turn_f": (28.05, 28.9, 27.53, 28.94),
        "route": (28.97, 30.6, 28.96, 29.3),
        "gates": (31.7, 32.46, 30.62, 36.53),
        "turn_w": (33.39, 33.14, 36.36, 41.31),
        "bias2": (39.95, 37.62, 36.92, 42.42),
    }
    LOW_W_AT, LOW_W_GAP = 65.76, 0.04
    steps_at = [(at, *step) for step, at in ONCE.items()]
    steps_at += [(LOW_W_AT + LOW_W_GAP * k, "low_w", k % 2, k // 2) for k in range(2 * NE)]
    steps_at += [(KEYS_AT[half][s], "keys", half, s) for half in range(2) for s in range(SL)]
    for b in range(B):
        t0 = UNITS * b
        steps_at += [(t0 + at[b], name, b, 0) for name, at in BATCH_AT.items()]
        for s in range(SL):
            done = t0 + (G + 1) * (s + 1)
            steps_at += [(t0 + QUERY_AT[b][s], "query", b, s), (t0 + MAXROWS_AT[b][s], "maxrows", b, s),
                         (done + TAKE_SUMS_AFTER[b], "take_sums", b, s), (done + NORMALISE_AFTER[b], "normalise", b, s)]
            steps_at += [(t0 + MAXIMA_AT[b][s] + MAXIMA_GAP[b] * n, "maxima", b, s * T * HALVES + n) for n in range(T * HALVES)]
        for k in range(UNITS):
            after_scores = SUMS_AFTER[b] if k % (G + 1) else REST_AFTER[b]
            steps_at += [(t0 + k, "scores", b, k), (t0 + k + after_scores, "sums", b, k)]

    def order(engine):
        parts = [(at + LAG[name][engine], n, (name, b, i)) for n, (at, name, b, i) in enumerate(steps_at) if engine in LAG[name]]
        return [step for _, _, step in sorted(parts)]

    SHARED_STEPS = ("turn_ctxA", "turn_ctxB", "columns", "maskrows", "spread", "keys", "valuesA", "valuesB", "turn_b1", "norm1",
                    "query", "maxrows", "normalise", "turn_o", "project", "turn_f", "route", "turn_w", "bias2")
    shared_use = {step: n for n, step in enumerate([st for st in order("PE") if st[0] in SHARED_STEPS])}

    stack = ExitStack()
    with stack:
        def sb(name, shape, dt=f32):
            return stack.enter_context(nc.sbuf_tensor(name, shape, dt))

        def sem(name):
            return stack.enter_context(nc.semaphore(name))

        xs = sb("xs", [128, NT, D])
        ctxA = sb("ctxA", [KA, B, D])
        ctxB = sb("ctxB", [KR, B, D])
        wq = sb("wq", [D, D])
        wk = sb("wk", [D, D])
        wv = sb("wv", [D, D])
        wo = sb("wo", [D, D])
        wr = sb("wr", [D, E])
        rows = sb("rows", [1, 2 * D + E])
        w1 = sb("w1", [D, NE, C * 128])
        w2 = sb("w2", [128, NE, C, D])
        b1r = sb("b1r", [NE * C, 128])
        b2 = sb("b2", [NE, D])
        ident = sb("ident", [128, 128])
        ones = sb("ones", [1, 128])
        tri = sb("tri", [128, E, E])
        masksel = sb("masksel", [128, 128])
        powc = sb("powc", [128, T])
        bqk = sb("bqk", [128, R])
        prow = sb("prow", [128, G, R])
        cols = sb("cols", [128, 4 * SL + 2])
        b1c = sb("b1c", [128, NE * C])
        bcur = sb("bcur", [128, C])
        boB = sb("boB", [128, D])
        rbB = sb("rbB", [128, E])
        wqS = sb("wqS", [D, SL, G, R])
        wkS = sb("wkS", [D, SL, G, R])
        wrh = sb("wrh", [D, E], f16)
        wrl = sb("wrl", [D, E], f16)
        w1h = sb("w1h", [D, NE, C * 128], f16)
        w1l = sb("w1l", [D, NE, C * 128], f16)
        w2h = sb("w2h", [128, NE, C, D], f16)
        w2l = sb("w2l", [128, NE, C, D], f16)
        ctxT = sb("ctxT", [D, B, KP])
        ctxT4 = sb("ctxT4", [D, B, G, KR])
        asum = sb("asum", [128, 2, B])
        maskcol = sb("maskcol", [128, 2, B])
        maskmat = sb("maskmat", [128, 2, B, 128])
        maskrows = sb("maskrows", [128, B, KP])
        khalf = sb("khalf", [128, 2, 2, KP], f16)
        krest = sb("krest", [128, 2, KP])
        kall = sb("kall", [128, 2, KP], f16)
        kd = sb("kd", [128, B, SL, G, KP], f16)
        kdr = sb("kdr", [128, B, SL, G, KR], f16)
        va = sb("va", [KA, B, H, R])
        vb = sb("vb", [128, B, SL, G, R])
        stats = sb("stats", [128, T, 6])
        meanvar = sb("meanvar", [128, T, 2])
        varp = sb("varp", [128, T])
        rstd = sb("rstd", [128, T])
        xn = sb("xn", [128, T, D])
        xnT = sb("xnT", [D, L])
        qhalf = sb("qhalf", [128, 2, L], f16)
        qs = sb("qs", [128, 2, SL, L], f16)
        mx = sb("mx", [128, SL, G, T])
        mneg = sb("mneg", [128, 2, G, T])
        maxT = sb("maxT", [G * T, 2, 128], f16)
        pr = sb("pr", [128, PR, L])
        oT = sb("oT", [128, 2, L])
        den = sb("den", [128, T, G])
        rden = sb("rden", [128, T, G])
        o = sb("o", [128, T, SL, G, DH])
        omT = sb("omT", [D, L])
        xb = sb("xb", [128, NT, D])
        stats2 = sb("stats2", [128, T, 6])
        meanvar2 = sb("meanvar2", [128, T, 2])
        varp2 = sb("varp2", [128, T])
        rstd2 = sb("rstd2", [128, T])
        xn2 = sb("xn2", [128, T, D])
        fh = sb("fh", [D, NT * 128], f16)
        fl = sb("fl", [D, NT * 128], f16)
        logits = sb("logits", [128, T, E])
        lmax = sb("lmax", [128, T])
        lsh = sb("lsh", [128, T, E])
        pexp = sb("pexp", [128, T, E])
        psum_e = sb("psum_e", [128, T])
        pinv = sb("pinv", [128, T])
        above = sb("above", [128, T, E, E])
        rank = sb("rank", [128, T, E])
        gate = sb("gate", [128, NT, NE])
        gate64 = sb("gate64", [128, NT, NE])
        gateT = sb("gateT", [NE, L])
        h32 = sb("h32", [128, 2, C, L])
        hh = sb("hh", [128, B, C, L], f16)
        hl = sb("hl", [128, B, C, L], f16)

        banks = stack.enter_context(nc.psum_tensor("banks", [128, 8, 512], f32))
        MAXBANKS, SCOREB, PVB, SHAREDB = 3, 4, 6, (3, 7)
        UPB = (0, 1, 2, 6)
        DOWNB = 4
        EARLYB = 2

        def tile_number(pos, g):
            return FIRST.index((pos, g)) if isinstance(pos, int) and (pos, g) in FIRST else pos * B + g

        def up_bank(n, c):
            return UPB[c if n < EARLY else 2 * (n % 2) + c]

        def down_bank(n):
            return EARLYB if n < EARLY else DOWNB + n % 2

        def shared(step):
            return banks[:, SHAREDB[shared_use[step] % 2], :]

        ctx_loaded, wk_loaded, wq_loaded, ffn_loaded = sem("ctx_loaded"), sem("wk_loaded"), sem("wq_loaded"), sem("ffn_loaded")
        x_loaded = [sem(f"x_loaded{b}") for b in range(B)]
        small_loaded, rows_loaded, rest_loaded = sem("small_loaded"), sem("rows_loaded"), sem("rest_loaded")
        ident_made, prow_ready, ctx4_ready = sem("ident_made"), sem("prow_ready"), sem("ctx4_ready")
        rstd1_ready, rstd2_ready = sem("rstd1_ready"), sem("rstd2_ready")
        pool_step, dve_step = sem("pool_step"), sem("dve_step")
        pads_zeroed, consts_made, keys_zeroed = sem("pads_zeroed"), sem("consts_made"), sem("keys_zeroed")
        values_padded, tri_made = sem("values_padded"), sem("tri_made")
        weights_padded = sem("weights_padded")
        shared_full = sem("shared_full")
        ctxT_ready, cols_ready, masks_ready, maskrows_ready = sem("ctxT_ready"), sem("cols_ready"), sem("masks_ready"), sem("maskrows_ready")
        spread_ready, khalf_ready, kall_ready, kd_ready = sem("spread_ready"), sem("khalf_ready"), sem("kall_ready"), sem("kd_ready")
        values_ready, b1c_ready, router_split = sem("values_ready"), sem("b1c_ready"), sem("router_split")
        residual_ready = sem("residual_ready")
        var1_ready, xn1_ready, xnT_ready = sem("var1_ready"), sem("xn1_ready"), sem("xnT_ready")
        qhalf_ready, qs_ready = sem("qhalf_ready"), sem("qs_ready")
        max_full, max_taken = sem("max_full"), sem("max_taken")
        mneg_ready, maxT_ready = sem("mneg_ready"), sem("maxT_ready")
        maxrow_sent = [sem("maxrow_sent0"), sem("maxrow_sent1")]
        score_full, exp_done, sums_done, oT_ready = sem("score_full"), sem("exp_done"), sem("sums_done"), sem("oT_ready")
        o_ready, omT_ready, x2_ready = sem("o_ready"), sem("omT_ready"), sem("x2_ready")
        var2_ready, xn2_ready, fh_ready, fl_ready = sem("var2_ready"), sem("xn2_ready"), sem("fh_ready"), sem("fl_ready")
        lsh_ready, pexp_ready, order_ready = sem("lsh_ready"), sem("pexp_ready"), sem("order_ready")
        gate_ready, gateT_ready, acc_ready = sem("gate_ready"), sem("gateT_ready"), sem("acc_ready")
        w64_ready, w_hi_ready, w_lo_ready = sem("w64_ready"), sem("w_hi_ready"), sem("w_lo_ready")
        up_full, gelu_done, hh_ready, hl_ready = sem("up_full"), sem("gelu_done"), sem("hh_ready"), sem("hl_ready")
        down_full, down_free, bias_taken = sem("down_full"), sem("down_free"), sem("bias_taken")
        stored = sem("stored")

        block = stack.enter_context(nc.Block())

        x_v = x.rearrange("b (t p) d -> p (b t) d", p=128)
        out_v = out.rearrange("b (t p) d -> p (b t) d", p=128)

        def row(v):
            return v.rearrange("(o n) -> o n", o=1)

        @block.sync
        def _(sp):
            sp.dma_start(ctxA[:, :, :], ctx_in[:, 0:KA, :].rearrange("b k d -> k b d")).then_inc(ctx_loaded, 16)
            sp.dma_start(xs[:, 0:T, :], x_v[:, 0:T, :]).then_inc(x_loaded[0], 16)
            sp.wait_ge(pads_zeroed, 1)
            sp.dma_start(ctxB[0:KB, :, :], ctx_in[:, KA:KEYS, :].rearrange("b k d -> k b d")).then_inc(ctx_loaded, 16)
            sp.dma_start(wv[:, :], Wv).then_inc(rows_loaded, 16)
            for k, v in enumerate((bv, bo)):
                sp.dma_start(rows[:, k * D:(k + 1) * D], row(v)).then_inc(rows_loaded, 16)
            sp.dma_start(rows[:, 2 * D:2 * D + E], row(router_b)).then_inc(rows_loaded, 16)
            for b in range(1, B):
                sp.dma_start(xs[:, b * T:(b + 1) * T, :], x_v[:, b * T:(b + 1) * T, :]).then_inc(x_loaded[b], 16)
            for name, b, s in order("SP"):
                n = b * SL + s
                sp.wait_ge(maxT_ready, n + 1)
                sp.dma_start(qs[MAXROW:128:R, b % 2, s, :].rearrange("g (t p) -> g t p", t=T), maxT[:, n % 2, :]).then_inc(maxrow_sent[n % 2], 16)
                if n == 0:
                    sp.dma_start(wo[:, :], Wo).then_inc(rest_loaded, 16)
                    sp.dma_start(wr[:, :], router_w).then_inc(rest_loaded, 16)
                    sp.dma_start(b1r[0:C, :], sb1.rearrange("(c p) -> c p", p=128)).then_inc(rest_loaded, 16)
                    sp.dma_start(b1r[C:NE * C, :], rb1.rearrange("e (c p) -> (e c) p", p=128)).then_inc(rest_loaded, 16)
                    sp.dma_start(b2[0:1, :], row(sb2)).then_inc(rest_loaded, 16)
                    sp.dma_start(b2[1:NE, :], rb2).then_inc(rest_loaded, 16)
                elif n == 1:
                    sp.dma_start(w1[:, 1:NE, :], rw1.rearrange("e d h -> d e h")).then_inc(ffn_loaded, 16)
                    sp.dma_start(w1[:, 0, :], sw1).then_inc(ffn_loaded, 16)
                    sp.dma_start(w2[:, 1:NE, :, :], rw2.rearrange("e (c p) d -> p e c d", p=128)).then_inc(ffn_loaded, 16)
                    sp.dma_start(w2[:, 0, :, :], sw2.rearrange("(c p) d -> p c d", p=128)).then_inc(ffn_loaded, 16)
            last = (NE - 1) * B
            for g in range(B):
                sp.wait_ge(down_free, last + g + 1)
                sp.dma_start(out_v[:, g * T:(g + 1) * T, :], xb[:, g * T:(g + 1) * T, :]).then_inc(stored, 16)
            sp.wait_ge(stored, 16 * B)

        @block.gpsimd
        def _(pool):
            steps = [0]

            def after(ins):
                steps[0] += 1
                ins.then_inc(pool_step, 1)
                pool.wait_ge(pool_step, steps[0])

            pool.memset(ctxB[:, :, :], 0.0).then_inc(pads_zeroed, 1)
            after(pool.memset(ident[:, :], 0.0))
            pool.affine_select(out=ident[:, :], in_=ident[:, :], compare_op=ALU.not_equal, fill=1.0, base=0,
                               pattern=[[-1, 128]], channel_multiplier=1).then_inc(ident_made, 1)
            pool.memset(wkS[:, :, :, :], 0.0)
            after(pool.memset(prow[:, :, :], 0.0))
            pool.memset(prow[0:SL, :, MASKROW:MASKROW + 1], BIG)
            pool.memset(prow[R:R + SL, :, MAXROW:MAXROW + 1], MAXUNIT)
            pool.memset(prow[2 * R:2 * R + 1, :, DH:2 * DH], 1.0)
            after(pool.memset(prow[3 * R:3 * R + 1, :, 2 * DH:3 * DH], 1.0))
            pool.memset(masksel[:, :], 0.0)
            after(pool.memset(wqS[:, :, :, :], 0.0))
            pool.memset(masksel[:, MASKROW:128:R], 1.0)
            after(pool.memset(powc[:, :], -0.5))
            pool.memset(ones[:, :], 1.0).then_inc(consts_made, 1)

            def rsqrt_norm(n, var_sem, v, r, mv, rows_in, b, to, done, power_done=None):
                pool.wait_ge(var_sem, n)
                power = pool.tensor_tensor(r[:, :], v[:, :], powc[:, :], ALU.pow)
                if power_done is not None:
                    power.then_inc(power_done, 1)
                    return
                after(power)
                after(pool.tensor_tensor(to[:, :, :], rows_in[:, b * T:(b + 1) * T, :], mv[:, :, 0:1].broadcast_to([128, T, D]),
                                         ALU.subtract))
                pool.tensor_tensor(to[:, :, :], to[:, :, :], r[:, :].unsqueeze(2).broadcast_to([128, T, D]),
                                   ALU.mult).then_inc(done, 1)

            padded = False
            for name, b, i in order("POOL"):
                if name == "stats1":
                    if b > 0:
                        pool.wait_ge(xnT_ready, b)
                    rsqrt_norm(b + 1, var1_ready, varp, rstd, meanvar, xs, b, xn, xn1_ready, rstd1_ready if b == 0 else None)
                elif name == "stats2":
                    if b > 0:
                        pool.wait_ge(fh_ready, b)
                    rsqrt_norm(b + 1, var2_ready, varp2, rstd2, meanvar2, xb, b, xn2, xn2_ready,
                               rstd2_ready if b == B - 1 else None)
                elif name == "residual":
                    pool.wait_ge(spread_ready, 1)
                    pool.wait_ge(x_loaded[b], 16)
                    for t in range(b * T, (b + 1) * T):
                        last = pool.tensor_tensor(xb[:, t, :], xs[:, t, :], boB[:, :], ALU.add)
                    last.then_inc(residual_ready, 1)
                elif name == "low_w":
                    w, wh, wl = ((w1, w1h, w1l), (w2, w2h, w2l))[b]
                    pool.wait_ge(w_hi_ready, b + 1)
                    pool.tensor_tensor(wl[:, i], w[:, i], wh[:, i], ALU.subtract).then_inc(w_lo_ready, 1)
                elif name == "route":
                    pool.wait_ge(pexp_ready, b + 1)
                    if b > 0:
                        pool.wait_ge(gate_ready, b)
                    p_e = pexp[:, :, :].unsqueeze(3).broadcast_to([128, T, E, E])
                    p_j = pexp[:, :, :].unsqueeze(2).broadcast_to([128, T, E, E])
                    pool.tensor_tensor(above[:, :, :, :], p_j, p_e, ALU.subtract).then_inc(order_ready, 1)
                if not padded:
                    padded = True
                    pool.memset(kdr[:, 2:4, :, :, :].bitcast(f32), 0.0)
                    pool.memset(kd[:, 2:4, :, :, :].bitcast(f32), 0.0).then_inc(keys_zeroed, 1)
                    pool.memset(va[:, :, :, :], 0.0)
                    after(pool.memset(vb[:, :, :, :, :], 0.0))
                    after(pool.memset(va[:, :, :, DH:DH + 1], 1.0))
                    for g in range(G):
                        after(pool.memset(vb[g * R:(g + 1) * R, :, :, g, DH:DH + 1], 1.0))
                    pool.memset(gate[:, :, 0:1], 1.0)
                    pool.memset(gate64[:, :, 0:1], 1.0 / WSCALE).then_inc(values_padded, 1)
                    after(pool.memset(tri[:, :, :], LEAST))
                    pool.affine_select(out=tri[:, :, :], in_=tri[:, :, :], compare_op=ALU.is_ge, fill=0.0, base=0,
                                       pattern=[[-1, E], [1, E]], channel_multiplier=0).then_inc(tri_made, 1)
                    pool.wait_ge(tri_made, 1)

        @block.scalar
        def _(act):
            act.dma_start(bqk[0:SL, :], bq.rearrange("(s r) -> s r", r=R)).then_inc(small_loaded, 16)
            act.dma_start(bqk[R:R + SL, :], bk.rearrange("(s r) -> s r", r=R)).then_inc(small_loaded, 16)
            act.dma_start(wk[:, :], Wk).then_inc(wk_loaded, 16)
            act.dma_start(wq[:, :], Wq).then_inc(wq_loaded, 16)

            lowQ = cols[:, 2 * SL:2 * SL + 1]
            lowK = cols[:, 2 * SL + 1:2 * SL + 2]

            def take_bias(pos):
                nc.scalar.activation(bcur[:, :], b1c[:, bass.ds(pos * C, C)], ACT.Copy).then_inc(bias_taken, 1)

            def gelu(pos, g):
                n = tile_number(pos, g)
                fixed = isinstance(pos, int)
                for c in range(C):
                    act.wait_ge(up_full, n * C + c + 1)
                    if c == 0 and not (fixed and n < 2):
                        act.wait_ge(hl_ready, n - 1)
                    bias = b1c[:, pos * C + c:pos * C + c + 1] if fixed else bcur[:, c:c + 1]
                    nc.scalar.activation(h32[:, n % 2 if fixed else g % 2, c, :], banks[:, up_bank(n if fixed else LOOPED * B + g, c), :],
                                         ACT.Gelu, scale=1.0 / WSCALE, bias=bias).then_inc(gelu_done, 1)
                act.wait_ge(gelu_done, n * C + C)
                if fixed and 0 < pos <= LOOPED:
                    act.wait_ge(down_full, tile_number(pos - 1, g) + 1)
                elif not (fixed and pos == 0):
                    act.wait_ge(down_full, n - B + 1)
                nc.scalar.activation(hh[:, g, :, :], h32[:, n % 2 if fixed else g % 2, :, :], ACT.Copy).then_inc(hh_ready, 1)

            for step in order("ACT"):
                name, b, i = step
                if name in SHARED_STEPS:
                    act.wait_ge(shared_full, shared_use[step] + 1)
                if name == "turn_ctxA":
                    act.activation(ctxT[:, :, 0:KA], shared(step).rearrange("p (b k) -> p b k", b=B), ACT.Copy).then_inc(ctxT_ready, 1)
                elif name == "turn_ctxB":
                    turned = shared(step)[:, 0:B * KR].rearrange("p (b k) -> p b k", b=B)
                    act.activation(ctxT[:, :, KA:KP], turned, ACT.Copy).then_inc(ctxT_ready, 1)
                elif name == "ctx4":
                    act.wait_ge(ctxT_ready, 2)
                    act.activation(ctxT4[:, :, :, :], ctxT[:, :, KA:KP].unsqueeze(2).broadcast_to([D, B, G, KR]),
                                   ACT.Copy).then_inc(ctx4_ready, 1)
                elif name == "pad_weights":
                    act.wait_ge(consts_made, 1)
                    for w, padded, loaded in ((wk, wkS, wk_loaded), (wq, wqS, wq_loaded)):
                        act.wait_ge(loaded, 16)
                        w_pad = padded[:, :, :, :].rearrange("p s g r -> p (s g) r")
                        for part in range(3):
                            last = act.activation(w_pad[:, :, part * DH:(part + 1) * DH],
                                                  w[:, :].rearrange("p (h d) -> p h d", d=DH), ACT.Copy)
                        last.then_inc(weights_padded, 1)
                elif name == "keys":
                    n = b * SL + i
                    act.wait_ge(cols_ready, 1)
                    if n >= 2:
                        act.wait_ge(kall_ready, n - 1)
                    act.activation(khalf[:, n % 2, :, :], shared(step)[:, 0:2 * KP].rearrange("p (b k) -> p b k", b=2),
                                   ACT.Identity, scale=lowK, bias=cols[:, 3 * SL + 2 + i:3 * SL + 3 + i]).then_inc(khalf_ready, 1)
                elif name == "valuesA":
                    act.wait_ge(values_padded, 1)
                    act.activation(va[:, :, :, :].rearrange("p b h r -> p (b h) r")[:, :, 0:DH],
                                   shared(step).rearrange("p (x d) -> p x d", d=DH), ACT.Copy).then_inc(values_ready, 1)
                elif name == "valuesB":
                    for g in range(G):
                        part = slice(g * R, (g + 1) * R)
                        last = act.activation(vb[part, :, :, :, :].rearrange("p b s g r -> p (b s) g r")[:, :, g, 0:DH],
                                              shared(step)[part, :].rearrange("p (x g d) -> p x g d", g=G, d=DH)[:, :, g, :], ACT.Copy)
                    last.then_inc(values_ready, 1)
                elif name == "norm1":
                    if b > 0:
                        act.wait_ge(shared_full, shared_use["query", b - 1, SL - 1] + 1)
                    act.activation(xnT[:, :], shared(step), ACT.Copy).then_inc(xnT_ready, 1)
                elif name == "query":
                    n = b * SL + i
                    act.wait_ge(cols_ready, 1)
                    if n >= 2:
                        act.wait_ge(qs_ready, n - 1)
                    act.activation(qhalf[:, n % 2, :], shared(step), ACT.Identity, scale=lowQ,
                                   bias=cols[:, 2 * SL + 2 + i:2 * SL + 3 + i]).then_inc(qhalf_ready, 1)
                elif name == "maxrows":
                    n = b * SL + i
                    if n >= 2:
                        act.wait_ge(maxrow_sent[n % 2], 16 * (n // 2))
                    act.activation(maxT[:, n % 2, :], shared(step)[0:G * T, 0:128], ACT.Copy).then_inc(maxT_ready, 1)
                elif name == "scores":
                    k = b * UNITS + i
                    act.wait_ge(score_full, k + 1)
                    if k >= PR:
                        act.wait_ge(sums_done, k - PR + 1)
                    act.activation(pr[:, k % PR, :], banks[:, SCOREB + k % 2, :], ACT.Exp, scale=SCALE).then_inc(exp_done, 1)
                elif name == "take_sums":
                    n = b * SL + i
                    act.wait_ge(sums_done, (n + 1) * (G + 1))
                    if n >= 2:
                        act.wait_ge(o_ready, n - 1)
                    act.activation(oT[:, n % 2, :], banks[:, PVB, :], ACT.Copy).then_inc(oT_ready, 1)
                elif name == "split_w":
                    w, wh = ((w1, w1h), (w2, w2h))[b]
                    act.wait_ge(ffn_loaded, 16 * 4)
                    act.activation(w[:], w[:], ACT.Copy, scale=WSCALE).then_inc(w64_ready, 1)
                    act.wait_ge(w64_ready, b + 1)
                    act.activation(wh[:], w[:], ACT.Copy).then_inc(w_hi_ready, 1)
                elif name == "turn_o":
                    act.activation(omT[:, :], shared(step), ACT.Copy).then_inc(omT_ready, 1)
                elif name == "turn_f":
                    act.activation(fh[:, b * L:(b + 1) * L], shared(step), ACT.Copy).then_inc(fh_ready, 1)
                elif name == "route":
                    act.wait_ge(lsh_ready, b + 1)
                    act.activation(pexp[:, :, :], lsh[:, :, :], ACT.Exp).then_inc(pexp_ready, 1)
                elif name == "turn_w":
                    if b > 0:
                        act.wait_ge(acc_ready, b)
                    act.activation(gateT[:, :], shared(step)[0:NE, :], ACT.Copy).then_inc(gateT_ready, 1)
                elif name == "up":
                    if i == 0:
                        act.wait_ge(b1c_ready, 1)
                    gelu(*FIRST[i])

            take_bias(LOOPED)
            act.wait_ge(bias_taken, 1)
            with act.Fori(LOOPED, NE - 1) as pos:
                gelu(pos, 2)
                gelu(pos, 3)
                take_bias(pos + 1)
                act.wait_ge(bias_taken, pos + (2 - LOOPED))
                gelu(pos + 1, 0)
                gelu(pos + 1, 1)
            gelu(NE - 1, 2)
            gelu(NE - 1, 3)

        @block.vector
        def _(dve):
            steps = [0]

            def after(ins):
                steps[0] += 1
                ins.then_inc(dve_step, 1)
                dve.wait_ge(dve_step, steps[0])

            def statistics(b, rows_in, stats, meanvar, varp, ready):
                for t in range(T):
                    last = nc.vector.bn_stats(stats[:, t, :], rows_in[:, b * T + t, :])
                after(last)
                for t in range(T):
                    last = nc.vector.bn_aggr(meanvar[:, t, :], stats[:, t, :])
                after(last)
                nc.vector.tensor_scalar(varp[:, :], meanvar[:, :, 1], EPS, None, ALU.add).then_inc(ready, 1)

            def low_parts(pos, g):
                n = tile_number(pos, g)
                dve.wait_ge(gelu_done, n * C + C)
                dve.wait_ge(hh_ready, n + 1)
                nc.vector.tensor_tensor(hl[:, g, :, :], h32[:, n % 2 if isinstance(pos, int) else g % 2, :, :], hh[:, g, :, :], ALU.subtract).then_inc(hl_ready, 1)

            def gated(pos, g):
                fixed = isinstance(pos, int)
                k = tile_number(pos, g)
                dve.wait_ge(down_full, k + 1)
                if fixed and pos == 0:
                    dve.wait_ge(acc_ready, g + 1)
                elif fixed and pos <= LOOPED:
                    dve.wait_ge(down_free, tile_number(pos - 1, g) + 1)
                bank = down_bank(k if fixed else LOOPED * B + g)
                for t in range(T):
                    n = g * T + t
                    last = nc.vector.scalar_tensor_tensor(xb[:, n, :], banks[:, bank, t * D:(t + 1) * D],
                                                          gate64[:, n, bass.ds(pos, 1)], xb[:, n, :], ALU.mult, ALU.add)
                last.then_inc(down_free, 1)

            nc.vector.memset(asum[:, :, :], 0.0)
            nc.vector.memset(cols[:, :], 0.0)
            nc.vector.memset(kd[:, 0:2, :, :, :].bitcast(f32), 0.0)
            after(nc.vector.memset(kdr[:, 0:2, :, :, :].bitcast(f32), 0.0))
            for step in order("DVE"):
                name, b, i = step
                if name in SHARED_STEPS and name != "maxrows":
                    dve.wait_ge(shared_full, shared_use[step] + 1)
                if name == "masks":
                    dve.wait_ge(ctx_loaded, 32)
                    nc.vector.tensor_reduce(asum[:, 0, :], ctxA[:, :, :], axis=AX.X, op=ALU.add, apply_absolute_value=True)
                    after(nc.vector.tensor_reduce(asum[0:KR, 1, :], ctxB[:, :, :], axis=AX.X, op=ALU.add, apply_absolute_value=True))
                    after(nc.vector.tensor_scalar(maskcol[:, :, :], asum[:, :, :], THRESHOLD, -BIG, ALU.is_le, ALU.mult))
                    dve.wait_ge(consts_made, 1)
                    for bb in range(B):
                        nc.vector.tensor_scalar(maskmat[:, 0, bb, :], masksel[:, :], maskcol[:, 0, bb:bb + 1], None, ALU.mult)
                        last = nc.vector.tensor_scalar(maskmat[0:KR, 1, bb, :], masksel[0:KR, :], maskcol[0:KR, 1, bb:bb + 1],
                                                       None, ALU.mult)
                    last.then_inc(masks_ready, 1)
                elif name == "pad_bias":
                    dve.wait_ge(consts_made, 1)
                    dve.wait_ge(small_loaded, 16 * 2)
                    for at in (0, R):
                        last = nc.vector.tensor_copy(prow[at:at + SL, :, 0:3 * DH].rearrange("s g (k d) -> s g k d", d=DH),
                                                     bqk[at:at + SL, :].rearrange("s (g d) -> s g d", d=DH)
                                                     .unsqueeze(2).broadcast_to([SL, G, 3, DH]))
                    last.then_inc(prow_ready, 1)
                elif name == "columns":
                    nc.vector.tensor_copy(cols[:, 0:SL], shared(step)[:, 0:SL])
                    nc.vector.tensor_copy(cols[:, SL:2 * SL], shared(step)[:, R:R + SL])
                    after(nc.vector.tensor_copy(cols[:, 2 * SL:2 * SL + 2], shared(step)[:, 2 * R:4 * R:R]))
                    nc.vector.tensor_scalar(cols[:, 2 * SL + 2:3 * SL + 2], cols[:, 0:SL], cols[:, 2 * SL:2 * SL + 1], None, ALU.mult)
                    nc.vector.tensor_scalar(cols[:, 3 * SL + 2:4 * SL + 2], cols[:, SL:2 * SL], cols[:, 2 * SL + 1:2 * SL + 2],
                                            None, ALU.mult).then_inc(cols_ready, 1)
                elif name == "maskrows":
                    nc.vector.tensor_copy(maskrows[:, 2 * b:2 * b + 2, :],
                                          shared(step)[:, 0:2 * KP].rearrange("p (b k) -> p b k", b=2)).then_inc(maskrows_ready, 1)
                elif name == "spread":
                    nc.vector.tensor_copy(rbB[:, :], shared(step)[:, D:D + E])
                    nc.vector.tensor_copy(boB[:, :], shared(step)[:, 0:D]).then_inc(spread_ready, 1)
                elif name == "keys":
                    n = b * SL + i
                    dve.wait_ge(khalf_ready, n + 1)
                    dve.wait_ge(maskrows_ready, b + 1)
                    after(nc.vector.scalar_tensor_tensor(krest[:, :, :], maskrows[:, 2 * b:2 * b + 2, :], cols[:, SL + i:SL + i + 1],
                                                         khalf[:, n % 2, :, :], ALU.add, ALU.subtract))
                    nc.vector.tensor_tensor(kall[:, :, :], shared(step)[:, 0:2 * KP].rearrange("p (b k) -> p b k", b=2),
                                            krest[:, :, :], ALU.add).then_inc(kall_ready, 1)
                    dve.wait_ge(kall_ready, n + 1)
                    if b == 1:
                        dve.wait_ge(keys_zeroed, 1)
                    for g in range(G):
                        part = slice(g * R, (g + 1) * R)
                        nc.vector.tensor_copy(kdr[part, 2 * b:2 * b + 2, i, g, :], kall[part, :, KA:KP])
                        last = nc.vector.tensor_copy(kd[part, 2 * b:2 * b + 2, i, g, :], kall[part, :, :])
                    last.then_inc(kd_ready, 1)
                elif name == "turn_b1":
                    nc.vector.tensor_copy(b1c[:, :], shared(step)[:, 0:NE * C]).then_inc(b1c_ready, 1)
                elif name == "split_router":
                    dve.wait_ge(rest_loaded, 16 * 6)
                    after(nc.vector.tensor_scalar(wr[:, :], wr[:, :], WSCALE, None, ALU.mult))
                    after(nc.vector.tensor_copy(wrh[:, :], wr[:, :]))
                    nc.vector.tensor_tensor(wrl[:, :], wr[:, :], wrh[:, :], ALU.subtract).then_inc(router_split, 1)
                elif name == "stats1":
                    dve.wait_ge(x_loaded[b], 16)
                    if b > 0:
                        dve.wait_ge(xn1_ready, b)
                    statistics(b, xs, stats, meanvar, varp, var1_ready)
                elif name in ("scale1", "scale2"):
                    mv, r, rows_in, to, power_done, done = {
                        "scale1": (meanvar, rstd, xs, xn, rstd1_ready, xn1_ready),
                        "scale2": (meanvar2, rstd2, xb, xn2, rstd2_ready, xn2_ready)}[name]
                    dve.wait_ge(power_done, 1)
                    for t in range(T):
                        last = nc.vector.tensor_scalar(to[:, t, :], rows_in[:, b * T + t, :], mv[:, t, 0:1], r[:, t:t + 1],
                                                       ALU.subtract, ALU.mult)
                    last.then_inc(done, 1)
                elif name == "query":
                    n = b * SL + i
                    dve.wait_ge(qhalf_ready, n + 1)
                    if b >= 2:
                        dve.wait_ge(score_full, (b - 2) * UNITS + (G + 1) * (i + 1))
                    nc.vector.scalar_tensor_tensor(qs[:, b % 2, i, :], shared(step), cols[:, i:i + 1], qhalf[:, n % 2, :],
                                                   ALU.add, ALU.subtract).then_inc(qs_ready, 1)
                elif name == "maxima":
                    n = b * SL * T * HALVES + i
                    s, t, c = i // (T * HALVES), i // HALVES % T, i % HALVES
                    dve.wait_ge(max_full, n + 1)
                    nc.vector.tensor_reduce(mx[:, s, 2 * c:2 * c + 2, t],
                                            banks[:, n % MAXBANKS, 0:2 * KEYS].rearrange("p (g k) -> p g k", k=KEYS),
                                            axis=AX.X, op=ALU.max).then_inc(max_taken, 1)
                elif name == "maxrows":
                    n = b * SL + i
                    dve.wait_ge(max_taken, (n + 1) * T * HALVES)
                    if n >= 2:
                        dve.wait_ge(maxT_ready, n - 1)
                    nc.vector.tensor_scalar(mneg[:, n % 2, :, :], mx[:, i, :, :], MAXFLOOR, -1.0 / MAXUNIT,
                                            ALU.max, ALU.mult).then_inc(mneg_ready, 1)
                elif name == "normalise":
                    turned = shared(step).rearrange("p (t g r) -> p t g r", g=G, r=R)
                    if i == 0 and b > 0:
                        dve.wait_ge(omT_ready, b)
                    after(nc.vector.tensor_scalar(den[:, :, :], turned[:, :, :, DH], 1e-30, None, ALU.max))
                    after(nc.vector.reciprocal(rden[:, :, :], den[:, :, :]))
                    nc.vector.tensor_tensor(o[:, :, i, :, :], turned[:, :, :, 0:DH],
                                            rden[:, :, :].unsqueeze(3).broadcast_to([128, T, G, DH]), ALU.mult).then_inc(o_ready, 1)
                elif name == "project":
                    dve.wait_ge(residual_ready, b + 1)
                    xr = xb[:, b * T:(b + 1) * T, :]
                    nc.vector.tensor_tensor(xr, shared(step).rearrange("p (t d) -> p t d", d=D), xr, ALU.add).then_inc(x2_ready, 1)
                elif name == "stats2":
                    dve.wait_ge(x2_ready, b + 1)
                    if b > 0:
                        dve.wait_ge(xn2_ready, b)
                    statistics(b, xb, stats2, meanvar2, varp2, var2_ready)
                elif name == "turn_f":
                    dve.wait_ge(fh_ready, b + 1)
                    nc.vector.tensor_tensor(fl[:, b * L:(b + 1) * L], shared(step), fh[:, b * L:(b + 1) * L],
                                            ALU.subtract).then_inc(fl_ready, 1)
                elif name == "route":
                    after(nc.vector.scalar_tensor_tensor(
                        logits[:, :, :], shared(step)[:, 0:T * E].rearrange("p (t e) -> p t e", e=E), 1.0 / WSCALE,
                        rbB[:, :].unsqueeze(1).broadcast_to([128, T, E]), ALU.mult, ALU.add))
                    after(nc.vector.tensor_reduce(lmax[:, :], logits[:, :, :], axis=AX.X, op=ALU.max))
                    nc.vector.tensor_tensor(lsh[:, :, :], logits[:, :, :], lmax[:, :].unsqueeze(2).broadcast_to([128, T, E]),
                                            ALU.subtract).then_inc(lsh_ready, 1)
                elif name == "gates":
                    dve.wait_ge(order_ready, b + 1)
                    dve.wait_ge(tri_made, 1)
                    after(nc.vector.tensor_tensor(above[:, :, :, :], above[:, :, :, :],
                                                  tri[:, :, :].unsqueeze(1).broadcast_to([128, T, E, E]), ALU.is_ge))
                    dve.wait_ge(values_padded, 1)
                    nc.vector.tensor_reduce(psum_e[:, :], pexp[:, :, :], axis=AX.X, op=ALU.add)
                    after(nc.vector.tensor_reduce(rank[:, :, :], above[:, :, :, :], axis=AX.X, op=ALU.add))
                    nc.vector.reciprocal(pinv[:, :], psum_e[:, :])
                    after(nc.vector.tensor_scalar(rank[:, :, :], rank[:, :, :], 1.5, None, ALU.is_lt))
                    after(nc.vector.tensor_tensor(rank[:, :, :], rank[:, :, :], pexp[:, :, :], ALU.mult))
                    gb = gate[:, b * T:(b + 1) * T, 1:NE]
                    after(nc.vector.tensor_tensor(gb, rank[:, :, :], pinv[:, :].unsqueeze(2).broadcast_to([128, T, E]), ALU.mult))
                    nc.vector.tensor_scalar(gate64[:, b * T:(b + 1) * T, 1:NE], gb, 1.0 / WSCALE, None, ALU.mult).then_inc(gate_ready, 1)
                elif name == "bias2":
                    xr = xb[:, b * T:(b + 1) * T, :]
                    nc.vector.tensor_tensor(xr, shared(step).rearrange("p (t d) -> p t d", d=D), xr, ALU.add).then_inc(acc_ready, 1)
                elif name == "up":
                    low_parts(*FIRST[i])
                elif name == "down":
                    gated(*FIRST[i])

            with dve.Fori(LOOPED, NE - 1) as pos:
                low_parts(pos, 2)
                gated(pos, 0)
                low_parts(pos, 3)
                gated(pos, 1)
                low_parts(pos + 1, 0)
                gated(pos, 2)
                low_parts(pos + 1, 1)
                gated(pos, 3)
            low_parts(NE - 1, 2)
            gated(NE - 1, 0)
            low_parts(NE - 1, 3)
            for g in range(1, B):
                gated(NE - 1, g)

        @block.tensor
        def _(pe):
            mm = nc.tensor.matmul

            read_by = {"turn_ctxA": ctxT_ready, "turn_ctxB": ctxT_ready, "columns": cols_ready, "maskrows": maskrows_ready,
                       "spread": spread_ready, "keys": kall_ready, "valuesA": values_ready, "valuesB": values_ready,
                       "turn_b1": b1c_ready, "norm1": xnT_ready, "query": qs_ready, "maxrows": maxT_ready, "normalise": o_ready,
                       "turn_o": omT_ready, "project": x2_ready, "turn_f": fl_ready, "route": lsh_ready, "turn_w": gateT_ready,
                       "bias2": acc_ready}
            counts = {}
            uses = []

            def turned(step, tiles, ins):
                for t in range(tiles):
                    src = ins(t)
                    width = src.free_size()
                    last = nc.tensor.transpose(shared(step)[0:width, t * 128:(t + 1) * 128], src, ident[:, :])
                last.then_inc(shared_full, 1)

            def up(pos, g):
                n = tile_number(pos, g) if isinstance(pos, int) else LOOPED * B + g
                for c in range(C):
                    to = banks[:, up_bank(n, c), :]
                    hi = w1h[:, bass.ds(pos, 1), c * 128:(c + 1) * 128]
                    lo = w1l[:, bass.ds(pos, 1), c * 128:(c + 1) * 128]
                    fhg, flg = fh[:, g * L:(g + 1) * L], fl[:, g * L:(g + 1) * L]
                    mm(to, hi, fhg, start=True, stop=False)
                    mm(to, hi, flg, start=False, stop=False)
                    mm(to, lo, fhg, start=False, stop=True).then_inc(up_full, 1)

            def down(pos, g, more=True):
                n = tile_number(pos, g)
                fixed = isinstance(pos, int)
                pe.wait_ge(hl_ready, n + 1)
                if fixed and 0 < n < EARLY:
                    pe.wait_ge(down_free, n)
                elif fixed and EARLY <= n < EARLY + 2:
                    pe.wait_ge(exp_done, B * UNITS)
                elif not (fixed and n == 0):
                    pe.wait_ge(down_free, n - 1)
                for t in range(T):
                    to = banks[:, down_bank(n if fixed else LOOPED * B + g), t * D:(t + 1) * D]
                    at = slice(t * 128, (t + 1) * 128)
                    if t == T - 1 and more:
                        pe.wait_ge(gelu_done, (n + 1) * C + C)
                    for c in range(C):
                        hi = w2h[:, bass.ds(pos, 1), c, :]
                        lo = w2l[:, bass.ds(pos, 1), c, :]
                        mm(to, hh[:, g, c, at], hi, start=c == 0, stop=False)
                        mm(to, hh[:, g, c, at], lo, start=False, stop=False)
                        last = mm(to, hl[:, g, c, at], hi, start=False, stop=c == C - 1)
                last.then_inc(down_full, 1)

            pe.wait_ge(ident_made, 1)
            for step in order("PE"):
                name, b, i = step
                if name in SHARED_STEPS:
                    n = shared_use[step]
                    if n >= 2:
                        pe.wait_ge(*uses[n - 2])
                    counts[read_by[name]] = counts.get(read_by[name], 0) + 1
                    uses.append((read_by[name], counts[read_by[name]]))
                if name == "turn_ctxA":
                    pe.wait_ge(ctx_loaded, 32)
                    turned(step, B, lambda t: ctxA[:, t, :])
                elif name == "turn_ctxB":
                    for bb in range(B):
                        last = nc.tensor.transpose(shared(step)[:, bb * KR:(bb + 1) * KR], ctxB[:, bb, :], ident[0:KR, 0:KR])
                    last.then_inc(shared_full, 1)
                elif name == "columns":
                    pe.wait_ge(prow_ready, 1)
                    turned(step, 1, lambda t: prow[:, :, :])
                elif name == "maskrows":
                    pe.wait_ge(masks_ready, 1)
                    for bb in range(2):
                        to = shared(step)[:, bb * KP:(bb + 1) * KP]
                        mm(to[:, 0:KA], maskmat[:, 0, 2 * b + bb, :], ident[:, :], start=True, stop=True)
                        last = mm(to[:, KA:KP], maskmat[0:KR, 1, 2 * b + bb, :], ident[0:KR, 0:KR], start=True, stop=True)
                    last.then_inc(shared_full, 1)
                elif name == "spread":
                    pe.wait_ge(rows_loaded, 16 * 4)
                    mm(shared(step)[:, 0:D], ones[0:1, :], rows[0:1, D:2 * D], start=True, stop=True)
                    mm(shared(step)[:, D:D + E], ones[0:1, :], rows[0:1, 2 * D:2 * D + E], start=True, stop=True).then_inc(shared_full, 1)
                elif name == "keys":
                    pe.wait_ge(weights_padded, 1)
                    pe.wait_ge(ctxT_ready, 2)
                    mm(shared(step)[:, 0:2 * KP], wkS[:, i, :, :], ctxT[:, 2 * b:2 * b + 2, :], start=True, stop=True)\
                        .then_inc(shared_full, 1)
                elif name in ("valuesA", "valuesB"):
                    pe.wait_ge(rows_loaded, 16 * 4)
                    pe.wait_ge(*((ctxT_ready, 2) if name == "valuesA" else (ctx4_ready, 1)))
                    for bb in range(B):
                        keys = ctxT[:, bb, 0:KA] if name == "valuesA" else ctxT4[:, bb, :, :]
                        to = shared(step)[:, bb * D:(bb + 1) * D]
                        mm(to, keys, wv[:, :], start=True, stop=False)
                        last = mm(to, ones[0:1, :], rows[0:1, 0:D], start=False, stop=True)
                    last.then_inc(shared_full, 1)
                elif name == "turn_b1":
                    pe.wait_ge(rest_loaded, 16 * 6)
                    nc.tensor.transpose(shared(step)[:, 0:NE * C], b1r[:, :], ident[0:NE * C, 0:NE * C]).then_inc(shared_full, 1)
                elif name == "norm1":
                    pe.wait_ge(xn1_ready, b + 1)
                    turned(step, T, lambda t: xn[:, t, :])
                elif name == "query":
                    pe.wait_ge(weights_padded, 2)
                    pe.wait_ge(xnT_ready, b + 1)
                    mm(shared(step), wqS[:, i, :, :], xnT[:, :], start=True, stop=True).then_inc(shared_full, 1)
                elif name == "maxima":
                    n = b * SL * T * HALVES + i
                    s, t, c = i // (T * HALVES), i // HALVES % T, i % HALVES
                    pe.wait_ge(qs_ready, b * SL + s + 1)
                    pe.wait_ge(kd_ready, b // 2 * SL + s + 1)
                    if n >= MAXBANKS:
                        pe.wait_ge(max_taken, n - MAXBANKS + 1)
                    mm(banks[:, n % MAXBANKS, 0:2 * KEYS], qs[:, b % 2, s, t * 128:(t + 1) * 128],
                       kd[:, b, s, 2 * c:2 * c + 2, 0:KEYS], start=True, stop=True).then_inc(max_full, 1)
                elif name == "maxrows":
                    n = b * SL + i
                    pe.wait_ge(mneg_ready, n + 1)
                    turned(step, 1, lambda t: mneg[:, n % 2, :, :])
                elif name == "scores":
                    k = b * UNITS + i
                    s, j = i // (G + 1), i % (G + 1)
                    n = b * SL + s
                    pe.wait_ge(maxrow_sent[n % 2], 16 * (n // 2 + 1))
                    if k >= 2:
                        pe.wait_ge(exp_done, k - 1)
                    keys = kdr[:, b, s, :, :] if j == 0 else kd[:, b, s, j - 1, 0:KA]
                    mm(banks[:, SCOREB + k % 2, :], keys, qs[:, b % 2, s, :], start=True, stop=True).then_inc(score_full, 1)
                elif name == "sums":
                    k = b * UNITS + i
                    s, j = i // (G + 1), i % (G + 1)
                    n = b * SL + s
                    pe.wait_ge(exp_done, k + 1)
                    if j == 0:
                        if n == 0:
                            pe.wait_ge(values_ready, 2)
                        else:
                            pe.wait_ge(oT_ready, n)
                        mm(banks[:, PVB, :], vb[:, b, s, :, :], pr[:, k % PR, :], start=True, stop=False,
                           skip_group_check=True).then_inc(sums_done, 1)
                    else:
                        g = j - 1
                        mm(banks[g * R:(g + 1) * R, PVB, :], va[:, b, s * G + g, :], pr[:, k % PR, :],
                           start=False, stop=True, skip_group_check=True).then_inc(sums_done, 1)
                elif name == "normalise":
                    n = b * SL + i
                    pe.wait_ge(oT_ready, n + 1)
                    turned(step, T, lambda t: oT[:, n % 2, t * 128:(t + 1) * 128])
                elif name == "turn_o":
                    pe.wait_ge(o_ready, (b + 1) * SL)
                    turned(step, T, lambda t: o[:, t, :, :, :])
                elif name == "project":
                    pe.wait_ge(omT_ready, b + 1)
                    pe.wait_ge(rest_loaded, 16 * 6)
                    for t in range(T):
                        last = mm(shared(step)[:, t * D:(t + 1) * D], omT[:, t * 128:(t + 1) * 128], wo[:, :], start=True, stop=True)
                    last.then_inc(shared_full, 1)
                elif name == "turn_f":
                    pe.wait_ge(xn2_ready, b + 1)
                    turned(step, T, lambda t: xn2[:, t, :])
                elif name == "route":
                    pe.wait_ge(fl_ready, b + 1)
                    pe.wait_ge(router_split, 1)
                    for t in range(T):
                        at = slice((b * T + t) * 128, (b * T + t + 1) * 128)
                        to = shared(step)[:, t * E:(t + 1) * E]
                        mm(to, fh[:, at], wrh[:, :], start=True, stop=False)
                        mm(to, fh[:, at], wrl[:, :], start=False, stop=False)
                        last = mm(to, fl[:, at], wrh[:, :], start=False, stop=True)
                    last.then_inc(shared_full, 1)
                elif name == "turn_w":
                    pe.wait_ge(gate_ready, b + 1)
                    turned(step, T, lambda t: gate[:, b * T + t, :])
                elif name == "bias2":
                    pe.wait_ge(gateT_ready, b + 1)
                    for t in range(T):
                        last = mm(shared(step)[:, t * D:(t + 1) * D], gateT[:, t * 128:(t + 1) * 128], b2[:, :], start=True, stop=True)
                    last.then_inc(shared_full, 1)
                elif name == "up":
                    pos, g = FIRST[i]
                    pe.wait_ge(w_lo_ready, 2 * NE if pos == LOOPED else 2 * pos + 1)
                    pe.wait_ge(fl_ready, g + 1)
                    if i == 0:
                        pe.wait_ge(max_taken, B * SL * T * HALVES)
                    elif i <= EARLY:
                        pe.wait_ge(gelu_done, C * i)
                    elif i == EARLY + 1:
                        pe.wait_ge(down_free, EARLY)
                        pe.wait_ge(oT_ready, B * SL)
                    else:
                        pe.wait_ge(gelu_done, C * (i - 1))
                    up(pos, g)
                elif name == "down":
                    pos, g = FIRST[i]
                    pe.wait_ge(w_lo_ready, 2 * pos + 2)
                    down(pos, g, more=i >= len(FIRST) - 4)

            with pe.Fori(LOOPED, NE - 1) as pos:
                up(pos, 2)
                down(pos, 0)
                up(pos, 3)
                down(pos, 1)
                up(pos + 1, 0)
                down(pos, 2)
                up(pos + 1, 1)
                down(pos, 3)
            up(NE - 1, 2)
            down(NE - 1, 0)
            up(NE - 1, 3)
            down(NE - 1, 1)
            down(NE - 1, 2)
            down(NE - 1, 3, more=False)


_INS = ['x', 'ctx_1024', 'L0_xattn_Wq', 'L0_xattn_bq', 'L0_xattn_Wk', 'L0_xattn_bk', 'L0_xattn_Wv', 'L0_xattn_bv',
        'L0_xattn_Wo', 'L0_xattn_bo', 'L0_ffn_router_w', 'L0_ffn_router_b', 'L0_ffn_sw1', 'L0_ffn_sb1', 'L0_ffn_sw2',
        'L0_ffn_sb2', 'L0_ffn_rw1', 'L0_ffn_rb1', 'L0_ffn_rw2', 'L0_ffn_rb2']


def kernel(**inputs):
    import numpy as np
    import concourse.bacc as bacc
    from concourse import mybir
    from concourse.bass_utils import run_bass_kernel_spmd

    nc = bacc.Bacc("TRN2", target_bir_lowering=False, num_devices=1)
    arrays, args = {}, []
    for name in _INS:
        a = np.ascontiguousarray(inputs[name])
        arrays[f"in_{name}"] = a
        args.append(nc.dram_tensor(f"in_{name}", a.shape, mybir.dt.from_np(a.dtype), kind="ExternalInput").ap())
    result = nc.dram_tensor("out_x", inputs["x"].shape, mybir.dt.float32, kind="ExternalOutput")
    xattn_moe_kernel(nc, *args, result.ap())
    r = run_bass_kernel_spmd(nc, [arrays], core_ids=[0])
    return r.results[0]["out_x"]
```
